# Optimizing a Trainium2 kernel written in Bass

```python
import numpy as np
import jax
import jax.numpy as jnp

def _softmax(x, axis=-1):
    return jax.nn.softmax(x, axis=axis)

def _gelu(x):
    return jax.nn.gelu(x, approximate=True)

def _silu(x):
    return jax.nn.silu(x)

def _sigmoid(x):
    return jax.nn.sigmoid(x)

def _layernorm(x, axis=-1, eps=1e-05):
    m = jnp.mean(x, axis=axis, keepdims=True)
    v = jnp.var(x, axis=axis, keepdims=True)
    return (x - m) / jnp.sqrt(v + eps)

def _scatter_add(tgt, idx, src, axis=0):
    return tgt.at[idx].add(src)

def _segment_sum(src, seg, n):
    return jax.ops.segment_sum(src, seg, n)
kernel_name = 'mk_gnn_preln_d1_gnn_r8_b88e6f'

def setup_inputs(seed: int=0):
    np.random.seed(seed)
    _w = jnp.asarray

    def _rec_inputs():
        import jax
        import jax.numpy as jnp
        _gk = jax.random.key(seed)
        x = -0.0005121 + 1.001 * jax.random.normal(jax.random.fold_in(_gk, 1), (12500, 64), jnp.float32)
        _s = jax.random.randint(jax.random.fold_in(_gk, 2), (100000,), 0, 12500, jnp.int32)
        _d = jax.random.randint(jax.random.fold_in(_gk, 3), (100000,), 0, 12500, jnp.int32)
        _loop = jnp.arange(12500, dtype=jnp.int32)
        src = jnp.concatenate([_s, _d, _loop])
        dst = jnp.concatenate([_d, _s, _loop])
        _o = jnp.argsort(dst, stable=True)
        src = src[_o]
        dst = dst[_o]
        edge_attr_64 = -9.77346e-05 + 0.999888 * jax.random.normal(jax.random.fold_in(_gk, 12), (212500, 64), jnp.float32)
        return (x, src, dst, edge_attr_64)
    x, src, dst, edge_attr_64 = _rec_inputs()

    def _L0_gnn_setup():
        import jax, jax.numpy as jnp
        import numpy as np
        N_NODES = 6250
        N_EDGES = 100000
        NODE_DIM = 64
        EDGE_DIM = 64
        OUT_DIM = 64
        key = jax.random.key(seed)
        ks = jax.random.split(key, 8)
        y = jax.random.normal(ks[0], (N_NODES, NODE_DIM), jnp.float32)
        edge_x = jax.random.normal(ks[1], (N_EDGES, EDGE_DIM), jnp.float32)
        src = jax.random.randint(ks[2], (N_EDGES,), 0, N_NODES, jnp.int32)
        dst = jax.random.randint(ks[3], (N_EDGES,), 0, N_NODES, jnp.int32)
        d_in = NODE_DIM + EDGE_DIM
        s = 1.0 / np.sqrt(d_in).astype(np.float32)
        W_pre = jax.random.uniform(ks[4], (d_in, d_in), jnp.float32, -s, s)
        b_pre = jax.random.uniform(ks[5], (d_in,), jnp.float32, -s, s)
        W_up = jax.random.uniform(ks[6], (d_in, OUT_DIM), jnp.float32, -s, s)
        b_up = jax.random.uniform(ks[7], (OUT_DIM,), jnp.float32, -s, s)
        return {'y': y, 'edge_x': edge_x, 'src': src, 'dst': dst, 'W_pre': W_pre, 'b_pre': b_pre, 'W_up': W_up, 'b_up': b_up}
    _L0_gnn_all = _L0_gnn_setup()
    _L0_gnn_in = {k: v for k, v in _L0_gnn_all.items() if k in ('W_pre', 'b_pre', 'W_up', 'b_up')}
    del _L0_gnn_all
    return {'x': x, 'src': src, 'dst': dst, 'edge_attr_64': edge_attr_64, 'L0_gnn_W_pre': _L0_gnn_in['W_pre'], 'L0_gnn_b_pre': _L0_gnn_in['b_pre'], 'L0_gnn_W_up': _L0_gnn_in['W_up'], 'L0_gnn_b_up': _L0_gnn_in['b_up']}

def reference(x, src, dst, edge_attr_64, L0_gnn_W_pre, L0_gnn_b_pre, L0_gnn_W_up, L0_gnn_b_up):
    import jax
    import jax.numpy as jnp

    def _L0_gnn_ref(y, edge_x, src, dst, W_pre, b_pre, W_up, b_up):
        import jax, jax.numpy as jnp
        import numpy as np
        N_NODES = 6250
        N_EDGES = 100000
        NODE_DIM = 64
        EDGE_DIM = 64
        OUT_DIM = 64
        msg_in = jnp.concatenate([y[src], edge_x], axis=1)
        msg = jax.nn.relu(msg_in @ W_pre + b_pre)
        num = y.shape[0]
        z_sum = jax.ops.segment_sum(msg, dst, num_segments=num)
        deg = jax.ops.segment_sum(jnp.ones(dst.shape, msg.dtype), dst, num_segments=num)
        z = z_sum / jnp.maximum(deg, 1.0)[:, None]
        h = jax.nn.relu(z @ W_up + b_up) + y
        return jnp.where(deg[:, None] > 0, h, y)
    h = jnp.maximum(_layernorm(x, axis=-1), 0.0)
    x = x + _L0_gnn_ref(h, edge_attr_64, src, dst, L0_gnn_W_pre, L0_gnn_b_pre, L0_gnn_W_up, L0_gnn_b_up)
    return x

_drawn_inputs = setup_inputs


def setup_inputs(seed=0):
    import zlib

    import numpy as np

    out = dict(_drawn_inputs(seed))
    spreads = {}
    factors = {'edge_attr_64': 3.412, 'L0_gnn_b_pre': 7.034}
    for name, (base, spread) in spreads.items():
        noise = np.random.default_rng([zlib.crc32(name.encode()), seed]).standard_normal(out[name].shape)
        drawn = base * np.exp(spread * noise) if base else spread * noise
        out[name] = jnp.asarray(drawn.astype(out[name].dtype))
    for name, factor in factors.items():
        out[name] = (out[name] * factor).astype(out[name].dtype)
    return out
```

```python
import concourse.bass as bass
from concourse import mybir
from contextlib import ExitStack



def gnn_kernel(nc, x, src, dst, edge, W_pre, b_pre, W_up, b_up, out):
    f32, bf16, i32 = mybir.dt.float32, mybir.dt.bfloat16, mybir.dt.int32
    ALU, ACT, AX = mybir.AluOpType, mybir.ActivationFunctionType, mybir.AxisListType

    N, D = x.shape
    E, DE = edge.shape
    F = D + DE
    P = 128
    EPS = 1e-5

    J = 4
    CHUNK = J * P
    CHUNKS = E // CHUNK
    U = 5
    STEPS = CHUNKS // U
    TAIL0 = CHUNKS * CHUNK
    TAIL = E - TAIL0
    WIN = 64
    assert STEPS * U == CHUNKS and STEPS <= P and 0 < TAIL <= P and F == P

    NP = 125
    NK = N // NP
    PIECES = 4
    KP = NK // PIECES
    assert NP * NK == N and PIECES * KP == NK

    GE = 125
    GT = E // GE
    GN = 500
    GB = -(-N // GN)
    assert GE * GT == E
    ACCW = max(GB * GN, N + WIN)

    FK = 5
    FSTEPS = NK // FK
    C = D + 1
    assert FSTEPS * FK == NK and FSTEPS % 2 == 0

    src_steps = src[0:TAIL0].rearrange("(i e) -> i e", i=STEPS)
    dst_steps = dst[0:TAIL0].rearrange("(i e) -> i e", i=STEPS)
    edge_chunks = edge[0:TAIL0, :].rearrange("(c p j) f -> c p j f", p=P, j=J)
    x_nodes = x.rearrange("(p k) f -> p k f", k=NK)
    out_nodes = out.rearrange("(p k) f -> p k f", k=NK)

    h_table = nc.dram_tensor("h_table", [N, D], f32)
    h_table_nodes = h_table.rearrange("(p k) f -> p k f", k=NK)

    with ExitStack() as ctx:
        def sb(name, shape, dt=f32):
            return ctx.enter_context(nc.sbuf_tensor(name, shape, dt))

        def sem(name):
            return ctx.enter_context(nc.semaphore(name))

        ident = sb("ident", [P, P])
        ones = sb("ones", [P, P])
        iota = sb("iota", [P, GN])
        eps = sb("eps", [P, 1])
        w_pre = sb("w_pre", [P, F])
        w_up = sb("w_up", [P, C])
        b_up_row = sb("b_up_row", [1, C])
        b_pre3 = sb("b_pre3", [3, F])
        b_rest = sb("b_rest", [3, F])
        b_high = sb("b_high", [3, F], bf16)
        b_mid = sb("b_mid", [3, F], bf16)
        b_low = sb("b_low", [3, F], bf16)
        b_split = sb("b_split", [3, F], bf16)
        ones3 = sb("ones3", [3, P], bf16)

        x_sb = sb("x_sb", [NP, NK, D])
        stats = sb("stats", [NP, NK, 6])
        m_sum = sb("m_sum", [NP, NK])
        m_dif = sb("m_dif", [NP, NK])
        var = sb("var", [NP, NK])
        rstd = sb("rstd", [NP, NK])
        shift = sb("shift", [NP, NK])
        late = sb("late", [P, NK * D])
        h_nodes = late[0:NP, :].rearrange("p (k f) -> p k f", k=NK)
        base_f = sb("base_f", [STEPS, U])
        acc = sb("acc", [P, 2, ACCW])

        src_int = acc[0:STEPS, 0, 0:U * CHUNK].bitcast(i32)
        dst_int = acc[0:STEPS, 0, U * CHUNK:2 * U * CHUNK].bitcast(i32)
        idx_f = sb("idx_f", [STEPS, U * CHUNK])
        src_cols = sb("src_cols", [P, STEPS + 1, U, J], i32)
        rel_cols = sb("rel_cols", [P, STEPS, U, J])
        base_row = sb("base_row", [1, CHUNKS + 1], i32)
        base_ok = sb("base_ok", [1, CHUNKS + 1], i32)
        ext = sb("ext", [STEPS, 2])
        outside = sb("outside", [STEPS, 2])
        n_outside_f = sb("n_outside_f", [1, 1])
        n_outside = sb("n_outside", [1, 1], i32)

        comb = [sb(f"comb{u}", [P, J, F]) for u in range(U)]
        src_idx = [sb(f"src_idx{u}", [P, J], i32) for u in range(U)]
        onehot = [sb(f"onehot{u}", [P, J, WIN]) for u in range(U)]
        comb_t = sb("comb_t", [F, J, P])
        msg = sb("msg", [P, J, F])

        tail_comb = sb("tail_comb", [TAIL, F])
        tail_src = sb("tail_src", [TAIL, 1], i32)
        tail_dst = sb("tail_dst", [TAIL, 2], i32)
        tail_dst_f = sb("tail_dst_f", [TAIL, 2])
        tail_rel = sb("tail_rel", [TAIL, 1])
        tail_out = sb("tail_out", [TAIL, 2])
        tail_onehot = sb("tail_onehot", [TAIL, WIN])

        g_dst = sb("g_dst", [GE, 1], i32)
        g_src = sb("g_src", [GE, 1], i32)
        g_dst_f = sb("g_dst_f", [GE, 1])
        g_onehot = comb[1][0:GE, :, :].rearrange("p j f -> p (j f)")[:, 0:GN]

        h_flat = late[:, :]
        at = 0
        sums, upd, res = [], [], []
        for s in range(2):
            sums.append(h_flat[:, at:at + 2 * FK * NP].rearrange("q (c k p) -> q c k p", c=2, k=FK))
            at += 2 * FK * NP
        for s in range(2):
            upd.append(h_flat[0:NP, at:at + FK * D].rearrange("p (k f) -> p k f", k=FK))
            at += FK * D
            res.append(h_flat[0:NP, at:at + FK * D].rearrange("p (k f) -> p k f", k=FK))
            at += FK * D
        assert at <= NK * D
        deg_max = [sb(f"deg_max{s}", [NP, FK]) for s in range(2)]
        deg_inv = [sb(f"deg_inv{s}", [NP, FK]) for s in range(2)]

        bank = [ctx.enter_context(nc.psum_tensor(f"bank{i}", [P, 512], f32)) for i in range(8)]
        ps_t = bank[0]
        ps_m = bank[1]
        ps_w = [bank[2], bank[3], bank[2], bank[3], bank[2]]
        ps_cnt = bank[4]
        ps_gz, ps_gd = bank[4], bank[5]
        ps_f = [bank[6], bank[7]]
        src_banks, dst_banks = bank[4:8], bank[0:4]

        x_in = [sem(f"x_in{g}") for g in range(PIECES)]
        src_in, dst_in, base_in, tail_in = sem("src_in"), sem("dst_in"), sem("base_in"), sem("tail_in")
        weights_in = sem("weights_in")
        consts_made, pool_prep = sem("consts_made"), sem("pool_prep")
        src_float, dst_rel = sem("src_float"), sem("dst_rel")
        idx_int_free = sem("idx_int_free")
        src_turned, rel_turned = sem("src_turned"), sem("rel_turned")
        src_cols_done, rel_cols_done = sem("src_cols_done"), sem("rel_cols_done")
        var_done, std_done, scale_done, h_done = sem("var_done"), sem("std_done"), sem("scale_done"), sem("h_done")
        h_stored, acc_zero = sem("h_stored"), sem("acc_zero")
        v_prep = sem("v_prep")
        bias_ready = sem("bias_ready")
        out_cols, counted, flag_ready = sem("out_cols"), sem("counted"), sem("flag_ready")
        edge_in = [sem(f"edge_in{u}") for u in range(U)]
        h_in = [sem(f"h_in{u}") for u in range(U)]
        src_idx_set, gathers_begun = sem("src_idx_set"), sem("gathers_begun")
        turned, evacuated, multiplied = sem("turned"), sem("evacuated"), sem("multiplied")
        msg_ready, onehot_ready, summed, added = sem("msg_ready"), sem("onehot_ready"), sem("summed"), sem("added")
        tail_h_in = sem("tail_h_in")
        g_in, g_h_in, g_turned, g_evac, g_mult = sem("g_in"), sem("g_h_in"), sem("g_turned"), sem("g_evac"), sem("g_mult")
        g_msg, g_hot, g_summed, g_added, g_dst_ready, g_next = (
            sem("g_msg"), sem("g_hot"), sem("g_summed"), sem("g_added"), sem("g_dst_ready"), sem("g_next"))
        acc_final = sem("acc_final")
        sums_ready, f_done, f_max, f_inv, upd_ready, res_ready = (
            sem("sums_ready"), sem("f_done"), sem("f_max"), sem("f_inv"), sem("upd_ready"), sem("res_ready"))
        stored = [sem("stored0"), sem("stored1")]

        DONE = CHUNKS + 1

        block = ctx.enter_context(nc.Block())

        @block.sync
        def _(sp):
            for g in range(PIECES):
                sp.dma_start(x_sb[:, g * KP:(g + 1) * KP, :], x_nodes[:, g * KP:(g + 1) * KP, :]).then_inc(x_in[g], 16)

            def load_edges(i, u):
                sp.dma_start(comb[u][:, :, D:F],
                             edge_chunks[bass.ds(i * U + u, 1), :, :, :].rearrange("c p j f -> (c p) j f")
                             ).then_inc(edge_in[u], 16)

            for u in range(U):
                load_edges(0, u)
            for g in range(PIECES):
                sp.wait_ge(h_done, g + 1)
                sp.dma_start(h_table_nodes[:, g * KP:(g + 1) * KP, :], h_nodes[:, g * KP:(g + 1) * KP, :]
                             ).then_inc(h_stored, 16)
            with sp.Fori(1, STEPS) as i:
                for u in range(U):
                    sp.wait_ge(turned, i * U + (u - U + 1))
                    load_edges(i, u)

            sp.wait_ge(flag_ready, 1)
            flag = sp.value_load(n_outside[0:1, 0:1], min_val=0, max_val=STEPS * 2 + TAIL * 2)
            with sp.If(flag > 0):
                with sp.Fori(0, GT) as t:
                    sp.wait_ge(g_next, t + 1)
                    sp.dma_start(g_dst[:, :], dst[bass.ds(t * GE, GE)].rearrange("(p a) -> p a", a=1)).then_inc(g_in, 16)
                    sp.dma_start(g_src[:, :], src[bass.ds(t * GE, GE)].rearrange("(p a) -> p a", a=1)).then_inc(g_in, 16)
                    sp.dma_start(comb[0][0:GE, 0, D:F], edge[bass.ds(t * GE, GE), :]).then_inc(g_in, 16)
            with sp.Else():
                sp.nop()

            with sp.Fori(0, FSTEPS // 2) as i:
                for s in range(2):
                    sp.wait_ge(res_ready, 2 * i + (s + 1))
                    sp.dma_start(out_nodes[:, bass.ds((2 * i + s) * FK, FK), :], res[s]).then_inc(stored[s], 16)
            for s in range(2):
                sp.wait_ge(stored[s], 16 * (FSTEPS // 2))

        @block.gpsimd
        def _(pool):
            steps = [0]

            def step(ins):
                steps[0] += 1
                ins.then_inc(pool_prep, 1)
                pool.wait_ge(pool_prep, steps[0])

            step(pool.memset(ident[:, :], 0.0))
            pool.affine_select(out=ident[:, :], in_=ident[:, :], compare_op=ALU.not_equal, fill=1.0,
                               base=0, pattern=[[-1, P]], channel_multiplier=1).then_inc(consts_made, 1)
            pool.memset(ones[:, :], 1.0).then_inc(consts_made, 1)
            pool.iota(iota[:, :], pattern=[[1, GN]], base=0, channel_multiplier=0,
                      allow_small_or_imprecise_dtypes=True).then_inc(consts_made, 1)
            pool.wait_ge(src_in, 16)
            pool.tensor_copy(idx_f[:, :], src_int).then_inc(src_float, 1)
            pool.wait_ge(dst_in, 16)
            pool.wait_ge(src_turned, 4)
            step(pool.tensor_copy(idx_f[:, :], dst_int))
            step(pool.tensor_copy(base_f[:, :], idx_f[:, :].rearrange("i (u e) -> i u e", u=U)[:, :, 0]))
            for u in range(U):
                part = idx_f[:, u * CHUNK:(u + 1) * CHUNK]
                pool.tensor_scalar(part, part, base_f[:, u:u + 1], None, ALU.subtract).then_inc(dst_rel, 1)
            pool.memset(acc[:, 1, :], 0.0).then_inc(acc_zero, 1)

            pool.wait_ge(h_stored, 16 * PIECES)

            def gather(u):
                pool.sem_inc(gathers_begun, 1)
                for j in range(J):
                    pool.indirect_dma_start(
                        out=comb[u][:, j, 0:D], out_offset=None, in_=h_table[:, :],
                        in_offset=bass.IndirectOffsetOnAxis(ap=src_idx[u][:, j:j + 1], axis=0),
                        bounds_check=N - 1).then_inc(h_in[u], 16)

            for u in range(U):
                pool.wait_ge(src_idx_set, u + 1)
                gather(u)
            with pool.Fori(1, STEPS) as i:
                for u in range(U):
                    pool.wait_ge(src_idx_set, i * U + (u + 1))
                    pool.wait_ge(turned, i * U + (u - U + 1))
                    gather(u)
            pool.wait_ge(tail_in, 16 * 4)
            pool.indirect_dma_start(
                out=tail_comb[:, 0:D], out_offset=None, in_=h_table[:, :],
                in_offset=bass.IndirectOffsetOnAxis(ap=tail_src[:, 0:1], axis=0),
                bounds_check=N - 1).then_inc(tail_h_in, 16)

            pool.wait_ge(flag_ready, 1)
            flag = pool.value_load(n_outside[0:1, 0:1], min_val=0, max_val=STEPS * 2 + TAIL * 2)
            with pool.If(flag > 0):
                with pool.Fori(0, GT) as t:
                    pool.wait_ge(g_in, 48 * t + 48)
                    pool.sem_inc(gathers_begun, 1)
                    pool.indirect_dma_start(
                        out=comb[0][0:GE, 0, 0:D], out_offset=None, in_=h_table[:, :],
                        in_offset=bass.IndirectOffsetOnAxis(ap=g_src[:, 0:1], axis=0),
                        bounds_check=N - 1).then_inc(g_h_in, 16)
            with pool.Else():
                pool.nop()

            def finish(i, s, first):
                pool.wait_ge(upd_ready, 2 * i + (s + 1))
                if not first:
                    pool.wait_ge(stored[s], 16 * i)
                pool.tensor_tensor(res[s], upd[s], x_sb[:, bass.ds((2 * i + s) * FK, FK), :],
                                   ALU.add).then_inc(res_ready, 1)

            for s in range(2):
                finish(0, s, True)
            with pool.Fori(1, FSTEPS // 2) as i:
                for s in range(2):
                    finish(i, s, False)

        @block.scalar
        def _(act):
            act.dma_start(src_int, src_steps).then_inc(src_in, 16)
            act.dma_start(dst_int, dst_steps).then_inc(dst_in, 16)
            act.dma_start(w_pre[:, :], W_pre).then_inc(weights_in, 16)
            act.dma_start(w_up[:, 0:D], W_up).then_inc(weights_in, 16)
            act.dma_start(b_up_row[:, 0:D], b_up.rearrange("(a f) -> a f", a=1)).then_inc(weights_in, 16)
            for q in range(3):
                act.dma_start(b_pre3[q:q + 1, :], b_pre.rearrange("(a f) -> a f", a=1)).then_inc(weights_in, 16)
            with nc.allow_non_contiguous_dma(reason="one index of each chunk"):
                act.dma_start(base_row[:, 0:CHUNKS],
                              dst[0:TAIL0].rearrange("(a c e) -> a c e", a=1, e=CHUNK)[:, :, 0]).then_inc(base_in, 16)
            act.dma_start(base_row[:, CHUNKS:CHUNKS + 1], dst[TAIL0:TAIL0 + 1].rearrange("(a b) -> a b", a=1)
                          ).then_inc(base_in, 16)
            act.dma_start(tail_src[:, :], src[TAIL0:E].rearrange("(p a) -> p a", a=1)).then_inc(tail_in, 16)
            act.dma_start(tail_dst[:, 0:1], dst[TAIL0:E].rearrange("(p a) -> p a", a=1)).then_inc(tail_in, 16)
            act.dma_start(tail_dst[:, 1:2], dst[TAIL0:TAIL0 + 1].rearrange("(p a) -> p a", a=1).broadcast_to([TAIL, 1])
                          ).then_inc(tail_in, 16)
            act.dma_start(tail_comb[:, D:F], edge[TAIL0:E, :]).then_inc(tail_in, 16)

            for g in range(PIECES):
                ks = slice(g * KP, (g + 1) * KP)
                act.wait_ge(var_done, g + 1)
                act.activation(rstd[:, ks], var[:, ks], ACT.Sqrt, scale=1.0 / D, bias=eps[0:NP, 0:1]).then_inc(std_done, 1)
            for g in range(PIECES):
                act.wait_ge(scale_done, g + 1)
                for k in range(g * KP, (g + 1) * KP):
                    last = act.activation(h_nodes[:, k, :], x_sb[:, k, :], ACT.Relu,
                                          scale=rstd[:, k:k + 1], bias=shift[:, k:k + 1])
                last.then_inc(h_done, 1)

            def set_src(i, u):
                act.activation(src_idx[u][:, :], src_cols[:, i, u, :], ACT.Copy).then_inc(src_idx_set, 1)

            act.wait_ge(src_cols_done, 4 + 1)
            for u in range(U):
                set_src(0, u)

            with act.Fori(0, STEPS) as i:
                for u in range(U):
                    act.wait_ge(h_in[u], 16 * J * i + 16 * J)
                    act.activation(src_idx[u][:, :], src_cols[:, bass.ds(i + 1, 1), u, :].rearrange("p a j -> p (a j)"),
                                   ACT.Copy).then_inc(src_idx_set, 1)
                    act.wait_ge(multiplied, i * U + (u + 1))
                    act.activation(msg[:, :, :], ps_m[:, :].rearrange("p (j f) -> p j f", j=J), ACT.Relu
                                   ).then_inc(msg_ready, 1)
            act.wait_ge(multiplied, DONE)
            act.activation(msg[0:TAIL, 0, :], ps_m[0:TAIL, 0:F], ACT.Relu).then_inc(msg_ready, 1)

            act.wait_ge(flag_ready, 1)
            flag = act.value_load(n_outside[0:1, 0:1], min_val=0, max_val=STEPS * 2 + TAIL * 2)
            with act.If(flag > 0):
                with act.Fori(0, GT) as t:
                    act.wait_ge(g_mult, t + 1)
                    act.activation(msg[0:GE, 0, :], ps_m[0:GE, 0:F], ACT.Relu).then_inc(g_msg, 1)
            with act.Else():
                act.nop()

            by_node = acc[:, :, 0:N].rearrange("q c (p k) -> q c k p", k=NK)

            def stage(i, s, first):
                if not first:
                    act.wait_ge(f_done, 2 * i + (s - 1))
                act.activation(sums[s], by_node[:, :, bass.ds((2 * i + s) * FK, FK), :], ACT.Copy
                               ).then_inc(sums_ready, 1)

            act.wait_ge(acc_final, 1)
            for s in range(2):
                stage(0, s, True)
            with act.Fori(1, FSTEPS // 2) as i:
                for s in range(2):
                    stage(i, s, False)

        @block.tensor
        def _(pe):
            pe.wait_ge(consts_made, 3)

            def turn_indices(banks, done):
                per_bank = U * J // 4
                for q in range(4):
                    for m in range(per_bank):
                        u, j = divmod(q * per_bank + m, J)
                        columns = idx_f[:, u * CHUNK + j:(u + 1) * CHUNK:J]
                        last = pe.transpose(banks[q][:, m * STEPS:(m + 1) * STEPS], columns, ident[0:STEPS, 0:STEPS])
                    last.then_inc(done, 1)

            pe.wait_ge(src_float, 1)
            turn_indices(src_banks, src_turned)
            pe.wait_ge(dst_rel, U)
            turn_indices(dst_banks, rel_turned)
            pe.wait_ge(weights_in, 16 * 6)
            pe.wait_ge(bias_ready, 1)
            pe.wait_ge(rel_cols_done, 4)

            def sum_window(m, p, hot, ps, done):
                for j in range(m):
                    pe.matmul(ps[:, 0:WIN], msg[0:p, j, :], hot(j), start=(j == 0), stop=(j == m - 1))
                for j in range(m):
                    last = pe.matmul(ps[:, WIN:2 * WIN], ones[0:p, :], hot(j), start=(j == 0), stop=(j == m - 1))
                last.then_inc(done, 1)

            def sum_chunk(u, n):
                pe.wait_ge(msg_ready, n + 1)
                pe.wait_ge(onehot_ready, n + 1)
                sum_window(J, P, lambda j: onehot[u][:, j, :], ps_w[u], summed)

            def multiply(j, p):
                pe.matmul(ps_m[0:p, j * F:(j + 1) * F], comb_t[:, j, 0:p], w_pre[:, :], start=True, stop=False)
                return pe.matmul(ps_m[0:p, j * F:(j + 1) * F], ones3[:, 0:p], b_split[:, :], start=False, stop=True)

            def chunk(i, u, first):
                n = i * U + u
                pe.wait_ge(edge_in[u], 16 * i + 16)
                pe.wait_ge(h_in[u], 16 * J * i + 16 * J)
                for j in range(J):
                    last = pe.transpose(ps_t[:, j * P:(j + 1) * P], comb[u][:, j, :], ident[:, :])
                last.then_inc(turned, 1)
                if not first:
                    if u >= 3 or not isinstance(i, int):
                        pe.wait_ge(added, n - (1 if u == 1 else 2))
                    sum_chunk((u - 1) % U, n - 1)
                pe.wait_ge(evacuated, n + 1)
                for j in range(J):
                    last = multiply(j, P)
                last.then_inc(multiplied, 1)

            for u in range(U):
                chunk(0, u, u == 0)
            with pe.Fori(1, STEPS) as i:
                for u in range(U):
                    chunk(i, u, False)

            pe.wait_ge(tail_in, 16 * 4)
            pe.wait_ge(tail_h_in, 16)
            pe.transpose(ps_t[:, 0:TAIL], tail_comb[:, :], ident[0:TAIL, 0:TAIL]).then_inc(turned, 1)
            pe.wait_ge(added, CHUNKS - 2)
            sum_chunk(U - 1, CHUNKS - 1)
            pe.wait_ge(evacuated, DONE)
            multiply(0, TAIL).then_inc(multiplied, 1)
            pe.wait_ge(msg_ready, DONE)
            pe.wait_ge(onehot_ready, DONE)
            pe.wait_ge(added, CHUNKS)
            sum_window(1, TAIL, lambda j: tail_onehot[:, :], ps_w[0], summed)

            pe.wait_ge(out_cols, 1)
            pe.matmul(ps_cnt[0:1, 0:2], ones[0:STEPS, 0:1], outside[:, :], start=True, stop=False)
            pe.matmul(ps_cnt[0:1, 0:2], ones[0:TAIL, 0:1], tail_out[:, :], start=False, stop=True).then_inc(counted, 1)

            pe.wait_ge(flag_ready, 1)
            flag = pe.value_load(n_outside[0:1, 0:1], min_val=0, max_val=STEPS * 2 + TAIL * 2)
            with pe.If(flag > 0):
                with pe.Fori(0, GT) as t:
                    pe.wait_ge(g_in, 48 * t + 48)
                    pe.wait_ge(g_h_in, 16 * t + 16)
                    pe.transpose(ps_t[:, 0:GE], comb[0][0:GE, 0, :], ident[0:GE, 0:GE]).then_inc(g_turned, 1)
                    pe.wait_ge(g_evac, t + 1)
                    multiply(0, GE).then_inc(g_mult, 1)
                    with pe.Fori(0, GB) as b:
                        pe.wait_ge(g_msg, t + 1)
                        pe.wait_ge(g_hot, t * GB + b + 1)
                        pe.matmul(ps_gz[:, 0:GN], msg[0:GE, 0, :], g_onehot, start=True, stop=True)
                        pe.matmul(ps_gd[:, 0:GN], ones[0:GE, :], g_onehot, start=True, stop=True).then_inc(g_summed, 1)
            with pe.Else():
                pe.nop()

            def project(i, s, first):
                pe.wait_ge(sums_ready, 2 * i + (s + 1))
                if not first:
                    pe.wait_ge(upd_ready, 2 * i + (s - 1))
                for k in range(FK):
                    o = ps_f[s][0:NP, k * C:(k + 1) * C]
                    pe.matmul(o, sums[s][:, 0, k, :], w_up[:, :], start=True, stop=False)
                    last = pe.matmul(o, sums[s][0:1, 1, k, :], b_up_row[:, :], start=False, stop=True)
                last.then_inc(f_done, 1)

            for s in range(2):
                project(0, s, True)
            with pe.Fori(1, FSTEPS // 2) as i:
                for s in range(2):
                    project(i, s, False)

        @block.vector
        def _(dve):
            steps = [0]

            def step(ins):
                steps[0] += 1
                ins.then_inc(v_prep, 1)
                dve.wait_ge(v_prep, steps[0])

            dve.memset(w_up[:, D:C], 0.0)
            dve.memset(b_up_row[:, D:C], 1.0)
            dve.memset(ones3[:, :], 1.0)
            dve.memset(src_cols[:, STEPS, :, :], 0).then_inc(src_cols_done, 1)
            step(dve.memset(eps[:, :], EPS))

            for g in range(PIECES):
                ks = slice(g * KP, (g + 1) * KP)
                dve.wait_ge(x_in[g], 16)
                for k in range(g * KP, (g + 1) * KP):
                    last = dve.bn_stats(stats[:, k, :], x_sb[:, k, :])
                step(last)
                dve.tensor_tensor(m_sum[:, ks], stats[:, ks, 1], stats[:, ks, 4], ALU.add)
                dve.tensor_tensor(m_dif[:, ks], stats[:, ks, 1], stats[:, ks, 4], ALU.subtract)
                step(dve.tensor_tensor(var[:, ks], stats[:, ks, 2], stats[:, ks, 5], ALU.add))
                step(dve.tensor_tensor(m_dif[:, ks], m_dif[:, ks], m_dif[:, ks], ALU.mult))
                dve.scalar_tensor_tensor(out=var[:, ks], in0=m_dif[:, ks], scalar=D / 4.0, in1=var[:, ks],
                                         op0=ALU.mult, op1=ALU.add).then_inc(var_done, 1)
            for g in range(PIECES):
                ks = slice(g * KP, (g + 1) * KP)
                dve.wait_ge(std_done, g + 1)
                step(dve.reciprocal(rstd[:, ks], rstd[:, ks]))
                dve.scalar_tensor_tensor(out=shift[:, ks], in0=m_sum[:, ks], scalar=-0.5, in1=rstd[:, ks],
                                         op0=ALU.mult, op1=ALU.mult).then_inc(scale_done, 1)

            def turned_columns(banks, done, cols, out_sem):
                per_bank = U * J // 4
                flat = cols.rearrange("p i u j -> p i (u j)")
                for q in range(4):
                    dve.wait_ge(done, q + 1)
                    dve.tensor_copy(flat[:, :, q * per_bank:(q + 1) * per_bank],
                                    banks[q][:, 0:per_bank * STEPS].rearrange("p (m i) -> p i m", m=per_bank)
                                    ).then_inc(out_sem, 1)

            turned_columns(src_banks, src_turned, src_cols[:, 0:STEPS, :, :], src_cols_done)

            dve.wait_ge(weights_in, 16 * 6)
            dve.wait_ge(consts_made, 3)
            step(dve.tensor_copy(b_high[:, :], b_pre3[:, :]))
            step(dve.tensor_tensor(b_rest[:, :], b_pre3[:, :], b_high[:, :], ALU.subtract))
            step(dve.tensor_copy(b_mid[:, :], b_rest[:, :]))
            step(dve.tensor_tensor(b_rest[:, :], b_rest[:, :], b_mid[:, :], ALU.subtract))
            step(dve.tensor_copy(b_low[:, :], b_rest[:, :]))
            step(dve.tensor_scalar(b_split[:, :], b_high[:, :], ident[0:3, 0:1], None, ALU.mult))
            step(dve.scalar_tensor_tensor(out=b_split[:, :], in0=b_mid[:, :], scalar=ident[0:3, 1:2], in1=b_split[:, :],
                                          op0=ALU.mult, op1=ALU.add))
            dve.scalar_tensor_tensor(out=b_split[:, :], in0=b_low[:, :], scalar=ident[0:3, 2:3], in1=b_split[:, :],
                                     op0=ALU.mult, op1=ALU.add).then_inc(bias_ready, 1)

            turned_columns(dst_banks, rel_turned, rel_cols, rel_cols_done)

            dve.wait_ge(base_in, 32)
            step(dve.tensor_scalar(base_ok[:, :], base_row[:, :], 0.0, float(N - 1), ALU.max, ALU.min))
            dve.wait_ge(tail_in, 16 * 4)
            step(dve.tensor_copy(tail_dst_f[:, :], tail_dst[:, :]))
            step(dve.tensor_tensor(tail_rel[:, :], tail_dst_f[:, 0:1], tail_dst_f[:, 1:2], ALU.subtract))
            step(dve.tensor_scalar(tail_onehot[:, :], iota[0:TAIL, 0:WIN], tail_rel[:, 0:1], None, ALU.is_equal))
            step(dve.memset(acc[:, 0, :], 0.0))
            dve.wait_ge(acc_zero, 1)
            dve.wait_ge(rel_cols_done, 4)

            def one_hot(i, u):
                rel = rel_cols[:, bass.ds(i, 1), u, :].rearrange("p a j -> p (a j)")
                dve.tensor_tensor(onehot[u][:, :, :],
                                  iota[:, 0:WIN].unsqueeze(1).broadcast_to([P, J, WIN]),
                                  rel.unsqueeze(2).broadcast_to([P, J, WIN]), ALU.is_equal).then_inc(onehot_ready, 1)

            def add_window(u, n, base):
                dve.wait_ge(summed, n + 1)
                if not isinstance(n, int):
                    dve.wait_ge(added, n)
                elif n > 0:
                    dve.wait_ge(added, n)
                at = acc[:, :, bass.ds(base, WIN)]
                dve.tensor_tensor(at, at, ps_w[u][:, 0:2 * WIN].rearrange("p (c w) -> p c w", c=2),
                                  ALU.add).then_inc(added, 1)

            def base_of(n):
                return dve.value_load(base_ok[0:1, bass.ds(n, 1)], min_val=0, max_val=N - 1)

            def chunk(i, u, first):
                n = i * U + u
                if not isinstance(i, int):
                    dve.wait_ge(summed, n - (U - 1))
                one_hot(i, u)
                dve.wait_ge(turned, n + 1)
                dve.tensor_copy(comb_t[:, :, :], ps_t[:, :].rearrange("p (j e) -> p j e", j=J)).then_inc(evacuated, 1)
                if not first:
                    add_window((u - 1) % U, n - 1, base_of(n - 1))

            for u in range(U):
                chunk(0, u, u == 0)
            with dve.Fori(1, STEPS) as i:
                for u in range(U):
                    chunk(i, u, False)

            dve.wait_ge(v_prep, steps[0])
            dve.wait_ge(turned, DONE)
            dve.tensor_copy(comb_t[:, 0, 0:TAIL], ps_t[:, 0:TAIL]).then_inc(evacuated, 1)
            add_window(U - 1, CHUNKS - 1, base_of(CHUNKS - 1))
            dve.sem_inc(onehot_ready, 1)

            step(dve.tensor_reduce(ext[:, 0:1], idx_f[:, :], AX.X, ALU.max))
            step(dve.tensor_reduce(ext[:, 1:2], idx_f[:, :], AX.X, ALU.min))
            dve.tensor_scalar(outside[:, 0:1], ext[:, 0:1], float(WIN), None, ALU.is_ge)
            dve.tensor_scalar(outside[:, 1:2], ext[:, 1:2], 0.0, None, ALU.is_lt)
            dve.tensor_scalar(tail_out[:, 0:1], tail_rel[:, :], float(WIN), None, ALU.is_ge)
            dve.tensor_scalar(tail_out[:, 1:2], tail_rel[:, :], 0.0, None, ALU.is_lt).then_inc(out_cols, 1)
            add_window(0, CHUNKS, base_of(CHUNKS))
            step(dve.tensor_tensor(x_sb[:, :, :], x_sb[:, :, :], h_nodes, ALU.add))
            dve.wait_ge(counted, 1)
            step(dve.tensor_reduce(n_outside_f[:, :], ps_cnt[0:1, 0:2], AX.X, ALU.add))
            dve.tensor_copy(n_outside[:, :], n_outside_f[:, :]).then_inc(flag_ready, 1)

            dve.wait_ge(flag_ready, 1)
            dve.wait_ge(added, DONE)
            flag = dve.value_load(n_outside[0:1, 0:1], min_val=0, max_val=STEPS * 2 + TAIL * 2)
            with dve.If(flag > 0):
                dve.memset(acc[:, :, :], 0.0).then_inc(g_next, 1)
                dve.wait_ge(g_next, 1)
                with dve.Fori(0, GT) as t:
                    dve.wait_ge(g_in, 48 * t + 48)
                    dve.tensor_copy(g_dst_f[:, :], g_dst[:, :]).then_inc(g_dst_ready, 1)
                    dve.wait_ge(g_turned, t + 1)
                    dve.tensor_copy(comb_t[:, 0, 0:GE], ps_t[:, 0:GE]).then_inc(g_evac, 1)
                    with dve.Fori(0, GB) as b:
                        m = t * GB + b
                        dve.wait_ge(g_dst_ready, m + t + 1)
                        dve.tensor_scalar(g_onehot, iota[0:GE, :], g_dst_f[:, 0:1], None, ALU.is_equal).then_inc(g_hot, 1)
                        dve.wait_ge(g_hot, m + 1)
                        dve.tensor_scalar(g_dst_f[:, :], g_dst_f[:, :], float(GN), None, ALU.subtract).then_inc(g_dst_ready, 1)
                        dve.wait_ge(g_summed, m + 1)
                        for c, ps in enumerate((ps_gz, ps_gd)):
                            at = acc[:, c, bass.ds(b * GN, GN)]
                            dve.tensor_tensor(at, at, ps[:, 0:GN], ALU.add).then_inc(g_added, 1)
                        dve.wait_ge(g_added, 2 * m + 2)
                    dve.sem_inc(g_next, 1)
            with dve.Else():
                dve.nop()
            dve.sem_inc(acc_final, 1)

            def scale(i, s, first):
                dve.wait_ge(f_done, 2 * i + (s + 1))
                o = ps_f[s][0:NP, 0:FK * C].rearrange("p (k c) -> p k c", k=FK)
                dve.tensor_scalar(deg_max[s][:, :], o[:, :, D], 1.0, None, ALU.max).then_inc(f_max, 1)
                dve.wait_ge(f_max, 2 * i + (s + 1))
                dve.reciprocal(deg_inv[s][:, :], deg_max[s][:, :]).then_inc(f_inv, 1)
                dve.wait_ge(f_inv, 2 * i + (s + 1))
                if not first:
                    dve.wait_ge(res_ready, 2 * i + (s - 1))
                dve.scalar_tensor_tensor(out=upd[s], in0=o[:, :, 0:D], scalar=0.0,
                                         in1=deg_inv[s][:, :].unsqueeze(2).broadcast_to([NP, FK, D]),
                                         op0=ALU.max, op1=ALU.mult).then_inc(upd_ready, 1)

            for s in range(2):
                scale(0, s, True)
            with dve.Fori(1, FSTEPS // 2) as i:
                for s in range(2):
                    scale(i, s, False)


_INS = ['x', 'src', 'dst', 'edge_attr_64', 'L0_gnn_W_pre', 'L0_gnn_b_pre', 'L0_gnn_W_up', 'L0_gnn_b_up']
_OUTS = [((12500, 64), 'float32')]


def kernel(**inputs):
    import numpy as _np
    import concourse.bacc as _bacc
    from concourse import mybir as _mybir
    from concourse.bass_utils import run_bass_kernel_spmd as _run

    nc = _bacc.Bacc("TRN2", target_bir_lowering=False, num_devices=1)
    arrays, args = {}, []
    for name in _INS:
        a = _np.ascontiguousarray(inputs[name])
        arrays[f"in_{name}_dram"] = a
        args.append(nc.dram_tensor(f"in_{name}_dram", a.shape, _mybir.dt.from_np(a.dtype), kind="ExternalInput").ap())
    for i, (shape, dtype) in enumerate(_OUTS):
        dt = _mybir.dt.from_np(_np.dtype(dtype))
        args.append(nc.dram_tensor(f"out_{i}_dram", shape, dt, kind="ExternalOutput").ap())
    gnn_kernel(nc, *args)
    r = _run(nc, [arrays], core_ids=[0])
    return r.results[0]["out_0_dram"]
```

```python
import concourse.bass as bass
from concourse import mybir
from contextlib import ExitStack



def gnn_kernel(nc, x, src, dst, edge, W_pre, b_pre, W_up, b_up, out):
    f32, bf16, i32 = mybir.dt.float32, mybir.dt.bfloat16, mybir.dt.int32
    ALU, ACT, AX = mybir.AluOpType, mybir.ActivationFunctionType, mybir.AxisListType

    N, D = x.shape
    E, DE = edge.shape
    F = D + DE
    P = 128
    EPS = 1e-5

    J = 4
    CHUNK = J * P
    CHUNKS = E // CHUNK
    U = 5
    STEPS = CHUNKS // U
    TAIL0 = CHUNKS * CHUNK
    TAIL = E - TAIL0
    WIN = 64
    assert STEPS * U == CHUNKS and STEPS <= P and 0 < TAIL <= P and F == P

    NP = 125
    NK = N // NP
    PIECES = 4
    KA, KG = 12, 4
    KP = NK // PIECES
    assert NP * NK == N and PIECES * KP == NK

    GE = 125
    GT = E // GE
    GN = 500
    GB = -(-N // GN)
    assert GE * GT == E
    ACCW = max(GB * GN, N + WIN)

    FP = 75
    FIN = 2 * FP
    LAG = 3
    LOOP_FIN = STEPS - LAG
    EXTRA = (N - LOOP_FIN * FIN) // (2 * NP)
    G_FIN = N // (2 * NP)
    assert LOOP_FIN * FIN + EXTRA * 2 * NP == N and G_FIN * 2 * NP == N
    C = D + 1

    src_steps = src[0:TAIL0].rearrange("(i e) -> i e", i=STEPS)
    dst_steps = dst[0:TAIL0].rearrange("(i e) -> i e", i=STEPS)
    edge_chunks = edge[0:TAIL0, :].rearrange("(c p j) f -> c p j f", p=P, j=J)
    x_nodes = x.rearrange("(p k) f -> p k f", k=NK)

    h_table = nc.dram_tensor("h_table", [N, D], f32)
    h_table_nodes = h_table.rearrange("(p k) f -> p k f", k=NK)

    with ExitStack() as ctx:
        def sb(name, shape, dt=f32):
            return ctx.enter_context(nc.sbuf_tensor(name, shape, dt))

        def sem(name):
            return ctx.enter_context(nc.semaphore(name))

        ident = sb("ident", [P, P])
        ones = sb("ones", [P, 1])
        iota = sb("iota", [P, GN])
        eps, eps_root = sb("eps", [P, 1]), sb("eps_root", [P, 1])
        w_pre = sb("w_pre", [P, F])
        w_up = sb("w_up", [P, C])
        b_neg = sb("b_neg", [P, F])
        b_col = sb("b_col", [F, 1])
        b_wide = sb("b_wide", [F, P])
        b_up_all = sb("b_up_all", [P, D])
        b_last = sb("b_last", [P, C])

        x_area = sb("x_area", [P, NK * D])
        x_sb = x_area[0:NP, :].rearrange("p (k f) -> p k f", k=NK)
        stats = sb("stats", [NP, NK, 6])
        m_sum = sb("m_sum", [NP, NK])
        m_dif = sb("m_dif", [NP, NK])
        var = sb("var", [NP, NK])
        rstd = sb("rstd", [NP, NK])
        shift = sb("shift", [NP, NK])
        h_nodes = sb("h_nodes", [NP, NK, D])
        base_f = sb("base_f", [STEPS, U])
        acc = sb("acc", [P, 2, ACCW])

        IDX = U * CHUNK
        src_f, dst_f = acc[0:STEPS, 0, 0:IDX], acc[0:STEPS, 0, IDX:2 * IDX]
        src_cols = sb("src_cols", [P, STEPS + 1, U, J], i32)
        rel_cols = sb("rel_cols", [P, STEPS, U, J])
        base_row = sb("base_row", [1, CHUNKS + 1], i32)
        base_ok = sb("base_ok", [1, CHUNKS + 1], i32)
        base_min = sb("base_min", [1, CHUNKS], i32)
        too_low = sb("too_low", [1, CHUNKS])
        n_low = sb("n_low", [1, 2])
        ext = sb("ext", [STEPS, 2])
        outside = sb("outside", [STEPS, 2])
        n_outside_f = sb("n_outside_f", [1, 1])
        n_outside = sb("n_outside", [1, 1], i32)

        comb = [sb(f"comb{u}", [P, J, F]) for u in range(U)]
        src_idx = [sb(f"src_idx{u}", [P, J], i32) for u in range(U)]
        onehot = [sb(f"onehot{u}", [P, J, WIN]) for u in range(U)]
        SLOT = [0, 1, 0, 1, 2]
        assert len(SLOT) == U
        comb_t = [sb(f"comb_t{b}", [F, J, P]) for b in range(3)]
        msg = [sb(f"msg{b}", [P, J, F]) for b in range(3)]
        deg_win = sb("deg_win", [P, WIN])

        tail_comb = sb("tail_comb", [TAIL, F])
        tail_src = sb("tail_src", [TAIL, 1], i32)
        tail_dst = sb("tail_dst", [TAIL, 2], i32)
        tail_dst_f = sb("tail_dst_f", [TAIL, 2])
        tail_rel = sb("tail_rel", [TAIL, 1])
        tail_out = sb("tail_out", [TAIL, 2])
        tail_onehot = sb("tail_onehot", [TAIL, WIN])

        g_dst = sb("g_dst", [GE, 1], i32)
        g_src = sb("g_src", [GE, 1], i32)
        g_dst_f = sb("g_dst_f", [GE, 1])
        g_onehot = comb[1][0:GE, :, :].rearrange("p j f -> p (j f)")[:, 0:GN]

        sums = x_area[:, 0:4 * NP].rearrange("q (c s p) -> q c s p", c=2, s=2)
        x_part, h_part, xh, upd, res = (
            x_area[0:NP, 4 * NP + 2 * D * q:4 * NP + 2 * D * (q + 1)].rearrange("p (s f) -> p s f", s=2)
            for q in range(5))
        deg_max = sb("deg_max", [NP, 2])
        deg_inv = sb("deg_inv", [NP, 2])

        bank = [ctx.enter_context(nc.psum_tensor(f"bank{i}", [P, 512], f32)) for i in range(8)]
        ps_t = bank[0:3]
        ps_m = bank[3:6]
        ps_w = bank[6]
        ps_cnt, ps_bias = bank[6], bank[3]
        ps_g = bank[6]
        ps_f = bank[7]
        src_banks, dst_banks = bank[0:4], bank[4:8]

        x_in = [sem(f"x_in{g}") for g in range(PIECES)]
        src_in, dst_in, base_in, tail_in, weights_in = (
            sem("src_in"), sem("dst_in"), sem("base_in"), sem("tail_in"), sem("weights_in"))
        consts_made, pool_prep, v_prep = sem("consts_made"), sem("pool_prep"), sem("v_prep")
        src_float, dst_float, dst_rel = sem("src_float"), sem("dst_float"), sem("dst_rel")
        src_turned, rel_turned = sem("src_turned"), sem("rel_turned")
        src_cols_done, rel_cols_done = sem("src_cols_done"), sem("rel_cols_done")
        var_done, std_done, scale_done = sem("var_done"), sem("std_done"), sem("scale_done")
        h_by_act, h_by_dve, h_by_pool, h_stored = sem("h_by_act"), sem("h_by_dve"), sem("h_by_pool"), sem("h_stored")
        acc_zero = sem("acc_zero")
        b_wide_made, bias_multiplied, bias_made = sem("b_wide_made"), sem("bias_multiplied"), sem("bias_made")
        out_cols, counted, flag_ready = sem("out_cols"), sem("counted"), sem("flag_ready")
        edge_in = [sem(f"edge_in{u}") for u in range(U)]
        h_in = [sem(f"h_in{u}") for u in range(U)]
        src_idx_set, gathers_begun = sem("src_idx_set"), sem("gathers_begun")
        turned, evacuated, multiplied = sem("turned"), sem("evacuated"), sem("multiplied")
        msg_ready, onehot_ready, summed, added = sem("msg_ready"), sem("onehot_ready"), sem("summed"), sem("added")
        deg_summed, deg_added = sem("deg_summed"), sem("deg_added")
        tail_h_in = sem("tail_h_in")
        g_in, g_h_in, g_turned, g_evac, g_mult = sem("g_in"), sem("g_h_in"), sem("g_turned"), sem("g_evac"), sem("g_mult")
        g_msg, g_hot, g_summed, g_added, g_dst_ready, g_next = (
            sem("g_msg"), sem("g_hot"), sem("g_summed"), sem("g_added"), sem("g_dst_ready"), sem("g_next"))
        part_in, staged, projected = sem("part_in"), sem("staged"), sem("projected")
        xh_made, f_max, f_inv, upd_made, res_ready, stored = (
            sem("xh_made"), sem("f_max"), sem("f_inv"), sem("upd_made"), sem("res_ready"), sem("stored"))
        g_acc_done = sem("g_acc_done")

        DONE = CHUNKS + 1
        FLAG_MAX = 2 * STEPS + 2 * TAIL + CHUNKS + 1

        def nodes_of(tensor, first, p):
            return tensor[bass.ds(first, 2 * p), :].rearrange("(s p) f -> p s f", s=2)

        def after_loop(k):
            return LOOP_FIN * FIN + (k - LOOP_FIN) * 2 * NP

        def node_piece(g):
            return slice(g * KP, (g + 1) * KP)

        block = ctx.enter_context(nc.Block())

        @block.sync
        def _(sp):
            for g in range(PIECES):
                sp.dma_start(x_sb[:, node_piece(g), :], x_nodes[:, node_piece(g), :]).then_inc(x_in[g], 16)

            def load_edges(i, u):
                sp.dma_start(comb[u][:, :, D:F],
                             edge_chunks[bass.ds(i * U + u, 1), :, :, :].rearrange("c p j f -> (c p) j f")
                             ).then_inc(edge_in[u], 16)

            for g in range(PIECES):
                sp.wait_ge(h_by_act, g + 1)
                sp.wait_ge(h_by_pool, g + 1)
                sp.wait_ge(h_by_dve, g + 1)
                sp.dma_start(h_table_nodes[:, node_piece(g), :], h_nodes[:, node_piece(g), :]).then_inc(h_stored, 16)
            for u in range(U):
                load_edges(0, u)

            def load_part(first, p):
                sp.dma_start(x_part[0:p, :, :], nodes_of(x, first, p)).then_inc(part_in, 16)
                sp.dma_start(h_part[0:p, :, :], nodes_of(h_table, first, p)).then_inc(part_in, 16)

            def store_result(k, first, p):
                sp.wait_ge(res_ready, k + 1)
                sp.dma_start(nodes_of(out, first, p), res[0:p, :, :]).then_inc(stored, 16)

            def loop_step(i, store, load):
                for u in range(U):
                    sp.wait_ge(turned, i * U + (u - U + 1))
                    load_edges(i, u)
                    if u == 0 and store:
                        store_result(i - (LAG + 1), (i - (LAG + 1)) * FIN, FP)
                    if u == 2 and load:
                        if store:
                            sp.wait_ge(stored, 16 * (i - LAG))
                        load_part((i - LAG) * FIN, FP)

            with sp.Fori(1, LAG) as i:
                loop_step(i, False, False)
            loop_step(LAG, False, True)
            with sp.Fori(LAG + 1, STEPS) as i:
                loop_step(i, True, True)
            last = LOOP_FIN - 1
            store_result(last, last * FIN, FP)
            for k in range(LOOP_FIN, LOOP_FIN + EXTRA):
                sp.wait_ge(stored, 16 * k)
                load_part(after_loop(k), NP)
                store_result(k, after_loop(k), NP)

            flag = sp.value_load(n_outside[0:1, 0:1], min_val=0, max_val=FLAG_MAX)
            sp.wait_ge(stored, 16 * (LOOP_FIN + EXTRA))
            with sp.If(flag > 0):
                with sp.Fori(0, GT) as t:
                    sp.wait_ge(g_next, t + 1)
                    sp.dma_start(g_dst[:, :], dst[bass.ds(t * GE, GE)].rearrange("(p a) -> p a", a=1)).then_inc(g_in, 16)
                    sp.dma_start(g_src[:, :], src[bass.ds(t * GE, GE)].rearrange("(p a) -> p a", a=1)).then_inc(g_in, 16)
                    sp.dma_start(comb[0][0:GE, 0, D:F], edge[bass.ds(t * GE, GE), :]).then_inc(g_in, 16)
                with sp.Fori(0, G_FIN) as b:
                    sp.wait_ge(stored, 16 * b + 16 * (LOOP_FIN + EXTRA))
                    load_part(b * 2 * NP, NP)
                    store_result(b + (LOOP_FIN + EXTRA), b * 2 * NP, NP)
                sp.wait_ge(stored, 16 * (LOOP_FIN + EXTRA + G_FIN))
            with sp.Else():
                sp.nop()

        @block.gpsimd
        def _(pool):
            steps = [0]

            def step(ins):
                steps[0] += 1
                ins.then_inc(pool_prep, 1)
                pool.wait_ge(pool_prep, steps[0])

            step(pool.memset(ident[:, :], 0.0))
            pool.affine_select(out=ident[:, :], in_=ident[:, :], compare_op=ALU.not_equal, fill=1.0,
                               base=0, pattern=[[-1, P]], channel_multiplier=1).then_inc(consts_made, 1)
            pool.iota(iota[:, :], pattern=[[1, GN]], base=0, channel_multiplier=0,
                      allow_small_or_imprecise_dtypes=True).then_inc(consts_made, 1)
            pool.iota(base_min[:, :], pattern=[[FIN, STEPS], [0, U]], base=-(LAG - 1) * FIN, channel_multiplier=0
                      ).then_inc(consts_made, 1)
            pool.memset(acc[:, 1, :], 0.0).then_inc(acc_zero, 1)

            def normalize(g):
                ks = slice(g * KP + KA, g * KP + KA + KG)
                pool.wait_ge(scale_done, g + 1)
                h = h_nodes[:, ks, :]
                step(pool.tensor_tensor(h, x_sb[:, ks, :], rstd[:, ks].unsqueeze(2).broadcast_to([NP, KG, D]), ALU.mult))
                step(pool.tensor_tensor(h, h, shift[:, ks].unsqueeze(2).broadcast_to([NP, KG, D]), ALU.add))
                pool.tensor_scalar(h, h, 0.0, None, ALU.max).then_inc(h_by_pool, 1)

            def relative(u):
                part = dst_f[:, u * CHUNK:(u + 1) * CHUNK]
                pool.tensor_scalar(part, part, base_f[:, u:u + 1], None, ALU.subtract).then_inc(dst_rel, 1)

            normalize(0)
            pool.wait_ge(dst_float, 1)
            step(pool.tensor_copy(base_f[:, :], dst_f.rearrange("i (u e) -> i u e", u=U)[:, :, 0]))
            relative(0)
            relative(1)
            normalize(1)
            relative(2)
            relative(3)
            normalize(2)
            normalize(3)
            relative(4)

            def gather(u):
                pool.sem_inc(gathers_begun, 1)
                for j in range(J):
                    pool.indirect_dma_start(
                        out=comb[u][:, j, 0:D], out_offset=None, in_=h_table[:, :],
                        in_offset=bass.IndirectOffsetOnAxis(ap=src_idx[u][:, j:j + 1], axis=0),
                        bounds_check=N - 1).then_inc(h_in[u], 16)

            pool.wait_ge(h_stored, 16 * PIECES)
            for u in range(U):
                pool.wait_ge(src_idx_set, u + 1)
                gather(u)
            with pool.Fori(1, STEPS) as i:
                for u in range(U):
                    pool.wait_ge(src_idx_set, i * U + (u + 1))
                    pool.wait_ge(turned, i * U + (u - U + 1))
                    gather(u)
            pool.wait_ge(tail_in, 16 * 4)
            pool.indirect_dma_start(
                out=tail_comb[:, 0:D], out_offset=None, in_=h_table[:, :],
                in_offset=bass.IndirectOffsetOnAxis(ap=tail_src[:, 0:1], axis=0),
                bounds_check=N - 1).then_inc(tail_h_in, 16)

            pool.wait_ge(flag_ready, 1)
            flag = pool.value_load(n_outside[0:1, 0:1], min_val=0, max_val=FLAG_MAX)
            with pool.If(flag > 0):
                with pool.Fori(0, GT) as t:
                    pool.wait_ge(g_in, 48 * t + 48)
                    pool.sem_inc(gathers_begun, 1)
                    pool.indirect_dma_start(
                        out=comb[0][0:GE, 0, 0:D], out_offset=None, in_=h_table[:, :],
                        in_offset=bass.IndirectOffsetOnAxis(ap=g_src[:, 0:1], axis=0),
                        bounds_check=N - 1).then_inc(g_h_in, 16)
            with pool.Else():
                pool.nop()

        @block.scalar
        def _(act):
            act.dma_start(src_f.bitcast(i32), src_steps).then_inc(src_in, 16)
            act.dma_start(dst_f.bitcast(i32), dst_steps).then_inc(dst_in, 16)
            act.dma_start(w_pre[:, :], W_pre).then_inc(weights_in, 16)
            act.dma_start(w_up[:, 0:D], W_up).then_inc(weights_in, 16)
            act.dma_start(b_up_all[:, :], b_up.rearrange("(a f) -> a f", a=1).broadcast_to([P, D])).then_inc(weights_in, 16)
            act.dma_start(b_neg[:, :], b_pre.rearrange("(a f) -> a f", a=1).broadcast_to([P, F])).then_inc(weights_in, 16)
            act.dma_start(b_col[:, :], b_pre.rearrange("(f a) -> f a", a=1)).then_inc(weights_in, 16)
            act.wait_ge(v_prep, 1)
            act.activation(eps_root[:, :], eps[:, :], ACT.Sqrt)
            act.wait_ge(src_in, 16)
            act.activation(src_f, src_f.bitcast(i32), ACT.Copy).then_inc(src_float, 1)

            for g in range(PIECES + 1):
                if g < PIECES:
                    ks = node_piece(g)
                    act.wait_ge(var_done, g + 1)
                    act.activation(rstd[:, ks], var[:, ks], ACT.Sqrt, scale=1.0 / D, bias=eps[0:NP, 0:1]
                                   ).then_inc(std_done, 1)
                if g == 0:
                    act.wait_ge(dst_in, 16)
                    act.activation(dst_f, dst_f.bitcast(i32), ACT.Copy).then_inc(dst_float, 1)
                else:
                    act.wait_ge(scale_done, g)
                    for k in range((g - 1) * KP, (g - 1) * KP + KA):
                        last = act.activation(h_nodes[:, k, :], x_sb[:, k, :], ACT.Relu,
                                              scale=rstd[:, k:k + 1], bias=shift[:, k:k + 1])
                    last.then_inc(h_by_act, 1)

            per_bank = U * J // 4
            src_flat = src_cols[:, 0:STEPS, :, :].rearrange("p i u j -> p i (u j)")
            for q in range(4):
                act.wait_ge(src_turned, q + 1)
                act.activation(src_flat[:, :, q * per_bank:(q + 1) * per_bank],
                               src_banks[q][:, 0:per_bank * STEPS].rearrange("p (m i) -> p i m", m=per_bank),
                               ACT.Copy).then_inc(src_cols_done, 1)
            act.wait_ge(src_cols_done, 4 + 1)
            for u in range(U):
                act.activation(src_idx[u][:, :], src_cols[:, 0, u, :], ACT.Copy).then_inc(src_idx_set, 1)
            with nc.allow_non_contiguous_dma(reason="one index of each chunk"):
                act.dma_start(base_row[:, 0:CHUNKS],
                              dst[0:TAIL0].rearrange("(a c e) -> a c e", a=1, e=CHUNK)[:, :, 0]).then_inc(base_in, 16)
            act.dma_start(base_row[:, CHUNKS:CHUNKS + 1], dst[TAIL0:TAIL0 + 1].rearrange("(a b) -> a b", a=1)
                          ).then_inc(base_in, 16)
            act.dma_start(tail_src[:, :], src[TAIL0:E].rearrange("(p a) -> p a", a=1)).then_inc(tail_in, 16)
            act.dma_start(tail_dst[:, 0:1], dst[TAIL0:E].rearrange("(p a) -> p a", a=1)).then_inc(tail_in, 16)
            act.dma_start(tail_dst[:, 1:2], dst[TAIL0:TAIL0 + 1].rearrange("(p a) -> p a", a=1).broadcast_to([TAIL, 1])
                          ).then_inc(tail_in, 16)
            act.dma_start(tail_comb[:, D:F], edge[TAIL0:E, :]).then_inc(tail_in, 16)

            def chunk(i, u):
                n = i * U + u
                act.wait_ge(turned, n + 1)
                act.activation(src_idx[u][:, :], src_cols[:, bass.ds(i + 1, 1), u, :].rearrange("p a j -> p (a j)"),
                               ACT.Copy).then_inc(src_idx_set, 1)
                if not isinstance(i, int) or u >= 2:
                    act.wait_ge(multiplied, n - 1)
                act.activation(comb_t[SLOT[u]][:, :, :], ps_t[SLOT[u]][:, :].rearrange("p (j e) -> p j e", j=J), ACT.Copy
                               ).then_inc(evacuated, 1)

            def stage(first, p):
                nodes = acc[:, :, bass.ds(first, 2 * p)].rearrange("q c (s p) -> q c s p", s=2)
                act.activation(sums[:, :, :, 0:p], nodes, ACT.Copy).then_inc(staged, 1)

            for u in range(U):
                chunk(0, u)
            with act.Fori(1, LAG) as i:
                for u in range(U):
                    chunk(i, u)
            with act.Fori(LAG, STEPS) as i:
                for u in range(U):
                    chunk(i, u)
                    if u == 2:
                        act.wait_ge(added, i * U)
                        act.wait_ge(deg_added, i * U)
                        stage((i - LAG) * FIN, FP)
            act.wait_ge(turned, DONE)
            act.activation(comb_t[SLOT[0]][:, 0, 0:TAIL], ps_t[SLOT[0]][:, 0:TAIL], ACT.Copy).then_inc(evacuated, 1)

            act.wait_ge(added, DONE)
            act.wait_ge(deg_added, DONE)
            for k in range(LOOP_FIN, LOOP_FIN + EXTRA):
                act.wait_ge(projected, k)
                stage(after_loop(k), NP)

            flag = act.value_load(n_outside[0:1, 0:1], min_val=0, max_val=FLAG_MAX)
            with act.If(flag > 0):
                with act.Fori(0, GT) as t:
                    act.wait_ge(g_turned, t + 1)
                    act.activation(comb_t[0][:, 0, 0:GE], ps_t[0][:, 0:GE], ACT.Copy).then_inc(g_evac, 1)
                with act.Fori(0, G_FIN) as b:
                    act.wait_ge(g_acc_done, 1)
                    act.wait_ge(projected, b + (LOOP_FIN + EXTRA))
                    stage(b * 2 * NP, NP)
            with act.Else():
                act.nop()

        @block.tensor
        def _(pe):
            pe.wait_ge(consts_made, 3)

            def turn_indices(values, banks, done):
                per_bank = U * J // 4
                for q in range(4):
                    for m in range(per_bank):
                        u, j = divmod(q * per_bank + m, J)
                        last = pe.transpose(banks[q][:, m * STEPS:(m + 1) * STEPS],
                                            values[:, u * CHUNK + j:(u + 1) * CHUNK:J], ident[0:STEPS, 0:STEPS])
                    last.then_inc(done, 1)

            pe.wait_ge(src_float, 1)
            turn_indices(src_f, src_banks, src_turned)
            pe.wait_ge(dst_rel, U)
            turn_indices(dst_f, dst_banks, rel_turned)
            pe.wait_ge(weights_in, 16 * 5)
            pe.wait_ge(b_wide_made, 1)
            pe.wait_ge(src_cols_done, 4 + 1)
            pe.matmul(ps_bias[:, 0:D], b_wide[:, :], w_up[:, 0:D], start=True, stop=True).then_inc(bias_multiplied, 1)
            pe.wait_ge(out_cols, 1)
            pe.wait_ge(rel_cols_done, 4)
            pe.matmul(ps_cnt[0:1, 0:2], ones[0:STEPS, 0:1], outside[:, :], start=True, stop=False)
            pe.matmul(ps_cnt[0:1, 0:2], ones[0:TAIL, 0:1], tail_out[:, :], start=False, stop=False)
            pe.matmul(ps_cnt[0:1, 0:2], ones[0:1, 0:1], n_low[:, :], start=False, stop=True).then_inc(counted, 1)
            pe.wait_ge(bias_made, 1)
            pe.wait_ge(flag_ready, 1)

            def turn(i, u):
                pe.wait_ge(edge_in[u], 16 * i + 16)
                pe.wait_ge(h_in[u], 16 * J * i + 16 * J)
                for j in range(J):
                    last = pe.transpose(ps_t[SLOT[u]][:, j * P:(j + 1) * P], comb[u][:, j, :], ident[:, :])
                last.then_inc(turned, 1)

            def multiply(u, n):
                pe.wait_ge(evacuated, n + 1)
                for j in range(J):
                    last = pe.matmul(ps_m[SLOT[u]][:, j * F:(j + 1) * F], comb_t[SLOT[u]][:, j, :], w_pre[:, :],
                                     start=True, stop=True)
                last.then_inc(multiplied, 1)

            def sum_window(u, n, first):
                pe.wait_ge(msg_ready, n + 1)
                pe.wait_ge(onehot_ready, n + 1)
                if not first:
                    pe.wait_ge(added, n)
                for j in range(J):
                    last = pe.matmul(ps_w[:, 0:WIN], msg[SLOT[u]][:, j, :], onehot[u][:, j, :],
                                     start=(j == 0), stop=(j == J - 1))
                last.then_inc(summed, 1)

            def project(p):
                for q in range(2):
                    o = ps_f[0:p, q * C:(q + 1) * C]
                    pe.matmul(o, sums[:, 0, q, 0:p], w_up[:, :], start=True, stop=False)
                    last = pe.matmul(o, sums[:, 1, q, 0:p], b_last[:, :], start=False, stop=True)
                last.then_inc(projected, 1)

            for u in range(U):
                turn(0, u)
                if u >= 1:
                    multiply(u - 1, u - 1)
                if u >= 2:
                    sum_window(u - 2, u - 2, u == 2)
            with pe.Fori(1, LAG) as i:
                for u in range(U):
                    n = i * U + u
                    turn(i, u)
                    multiply((u - 1) % U, n - 1)
                    sum_window((u - 2) % U, n - 2, False)
            with pe.Fori(LAG, STEPS) as i:
                for u in range(U):
                    n = i * U + u
                    turn(i, u)
                    multiply((u - 1) % U, n - 1)
                    sum_window((u - 2) % U, n - 2, False)
                    if u == 3:
                        pe.wait_ge(staged, i - (LAG - 1))
                        project(FP)

            pe.wait_ge(tail_in, 16 * 4)
            pe.wait_ge(tail_h_in, 16)
            pe.transpose(ps_t[SLOT[0]][:, 0:TAIL], tail_comb[:, :], ident[0:TAIL, 0:TAIL]).then_inc(turned, 1)
            multiply(U - 1, CHUNKS - 1)
            sum_window(U - 2, CHUNKS - 2, False)
            pe.wait_ge(evacuated, DONE)
            pe.matmul(ps_m[SLOT[0]][0:TAIL, 0:F], comb_t[SLOT[0]][:, 0, 0:TAIL], w_pre[:, :], start=True, stop=True
                      ).then_inc(multiplied, 1)
            sum_window(U - 1, CHUNKS - 1, False)
            pe.wait_ge(msg_ready, DONE)
            pe.wait_ge(added, CHUNKS)
            pe.matmul(ps_w[:, 0:WIN], msg[SLOT[0]][0:TAIL, 0, :], tail_onehot[:, :], start=True, stop=True
                      ).then_inc(summed, 1)

            for k in range(LOOP_FIN, LOOP_FIN + EXTRA):
                pe.wait_ge(staged, k + 1)
                pe.wait_ge(upd_made, k)
                project(NP)

            flag = pe.value_load(n_outside[0:1, 0:1], min_val=0, max_val=FLAG_MAX)
            with pe.If(flag > 0):
                with pe.Fori(0, GT) as t:
                    pe.wait_ge(g_in, 48 * t + 48)
                    pe.wait_ge(g_h_in, 16 * t + 16)
                    pe.transpose(ps_t[0][:, 0:GE], comb[0][0:GE, 0, :], ident[0:GE, 0:GE]).then_inc(g_turned, 1)
                    pe.wait_ge(g_evac, t + 1)
                    pe.matmul(ps_m[0][0:GE, 0:F], comb_t[0][:, 0, 0:GE], w_pre[:, :], start=True, stop=True
                              ).then_inc(g_mult, 1)
                    with pe.Fori(0, GB) as b:
                        pe.wait_ge(g_msg, t + 1)
                        pe.wait_ge(g_hot, t * GB + b + 1)
                        pe.matmul(ps_g[:, 0:GN], msg[0][0:GE, 0, :], g_onehot, start=True, stop=True).then_inc(g_summed, 1)
                with pe.Fori(0, G_FIN) as b:
                    pe.wait_ge(staged, b + (LOOP_FIN + EXTRA + 1))
                    pe.wait_ge(upd_made, b + (LOOP_FIN + EXTRA))
                    project(NP)
            with pe.Else():
                pe.nop()

        @block.vector
        def _(dve):
            steps = [0]

            def step(ins):
                steps[0] += 1
                ins.then_inc(v_prep, 1)
                dve.wait_ge(v_prep, steps[0])

            dve.memset(w_up[:, D:C], 0.0)
            dve.memset(b_last[:, D:C], 1.0)
            dve.memset(ones[:, :], 1.0)
            dve.memset(src_cols[:, STEPS, :, :], 0).then_inc(src_cols_done, 1)
            step(dve.memset(eps[:, :], EPS))

            def statistics(g):
                ks = node_piece(g)
                dve.wait_ge(x_in[g], 16)
                for k in range(g * KP, (g + 1) * KP):
                    last = dve.bn_stats(stats[:, k, :], x_sb[:, k, :])
                step(last)
                dve.tensor_tensor(m_sum[:, ks], stats[:, ks, 1], stats[:, ks, 4], ALU.add)
                dve.tensor_tensor(m_dif[:, ks], stats[:, ks, 1], stats[:, ks, 4], ALU.subtract)
                step(dve.tensor_tensor(var[:, ks], stats[:, ks, 2], stats[:, ks, 5], ALU.add))
                step(dve.tensor_tensor(m_dif[:, ks], m_dif[:, ks], m_dif[:, ks], ALU.mult))
                dve.scalar_tensor_tensor(out=var[:, ks], in0=m_dif[:, ks], scalar=D / 4.0, in1=var[:, ks],
                                         op0=ALU.mult, op1=ALU.add).then_inc(var_done, 1)

            def normalize(g):
                ks = node_piece(g)
                mine = slice(g * KP + KA + KG, (g + 1) * KP)
                dve.wait_ge(std_done, g + 1)
                step(dve.reciprocal(rstd[:, ks], rstd[:, ks]))
                dve.scalar_tensor_tensor(out=shift[:, ks], in0=m_sum[:, ks], scalar=-0.5, in1=rstd[:, ks],
                                         op0=ALU.mult, op1=ALU.mult).then_inc(scale_done, 1)
                dve.wait_ge(scale_done, g + 1)
                for k in range(g * KP + KA + KG, (g + 1) * KP):
                    last = dve.tensor_scalar(h_nodes[:, k, :], x_sb[:, k, :], rstd[:, k:k + 1], shift[:, k:k + 1],
                                             ALU.mult, ALU.add)
                step(last)
                dve.tensor_scalar(h_nodes[:, mine, :], h_nodes[:, mine, :], 0.0, None, ALU.max).then_inc(h_by_dve, 1)

            for g in range(PIECES + 1):
                if g < PIECES:
                    statistics(g)
                if g > 0:
                    normalize(g - 1)

            dve.wait_ge(dst_rel, U)
            step(dve.tensor_reduce(ext[:, 0:1], dst_f, AX.X, ALU.max))
            step(dve.tensor_reduce(ext[:, 1:2], dst_f, AX.X, ALU.min))
            dve.tensor_scalar(outside[:, 0:1], ext[:, 0:1], float(WIN), None, ALU.is_ge)
            dve.tensor_scalar(outside[:, 1:2], ext[:, 1:2], 0.0, None, ALU.is_lt)
            per_bank = U * J // 4
            rel_flat = rel_cols[:, :, :, :].rearrange("p i u j -> p i (u j)")
            for q in range(4):
                dve.wait_ge(rel_turned, q + 1)
                dve.tensor_copy(rel_flat[:, :, q * per_bank:(q + 1) * per_bank],
                                dst_banks[q][:, 0:per_bank * STEPS].rearrange("p (m i) -> p i m", m=per_bank)
                                ).then_inc(rel_cols_done, 1)
            dve.wait_ge(rel_cols_done, 4)
            dve.wait_ge(consts_made, 3)
            dve.wait_ge(tail_in, 16 * 4)
            step(dve.tensor_copy(tail_dst_f[:, :], tail_dst[:, :]))
            step(dve.tensor_tensor(tail_rel[:, :], tail_dst_f[:, 0:1], tail_dst_f[:, 1:2], ALU.subtract))
            dve.tensor_scalar(tail_out[:, 0:1], tail_rel[:, :], float(WIN), None, ALU.is_ge)
            dve.tensor_scalar(tail_out[:, 1:2], tail_rel[:, :], 0.0, None, ALU.is_lt)
            dve.wait_ge(base_in, 32)
            dve.tensor_tensor(too_low[:, :], base_row[:, 0:CHUNKS], base_min[:, :], ALU.is_lt)
            step(dve.tensor_scalar(base_ok[:, :], base_row[:, :], 0.0, float(N - 1), ALU.max, ALU.min))
            dve.tensor_scalar(n_low[:, 1:2], base_row[:, CHUNKS:CHUNKS + 1], float(LOOP_FIN * FIN), None, ALU.is_lt)
            dve.tensor_reduce(n_low[:, 0:1], too_low[:, :], AX.X, ALU.add).then_inc(out_cols, 1)
            step(dve.tensor_scalar(tail_onehot[:, :], iota[0:TAIL, 0:WIN], tail_rel[:, 0:1], None, ALU.is_equal))
            dve.wait_ge(weights_in, 16 * 5)
            dve.tensor_copy(b_wide[:, :], b_col[:, 0:1].broadcast_to([F, P])).then_inc(b_wide_made, 1)
            step(dve.tensor_scalar(b_neg[:, :], b_neg[:, :], -1.0, None, ALU.mult))
            dve.wait_ge(bias_multiplied, 1)
            dve.tensor_tensor(b_last[:, 0:D], ps_bias[:, 0:D], b_up_all[:, :], ALU.add).then_inc(bias_made, 1)
            dve.wait_ge(counted, 1)
            step(dve.tensor_reduce(n_outside_f[:, :], ps_cnt[0:1, 0:2], AX.X, ALU.add))
            dve.tensor_copy(n_outside[:, :], n_outside_f[:, :]).then_inc(flag_ready, 1)
            dve.wait_ge(src_turned, 4)
            step(dve.memset(acc[:, 0, :], 0.0))
            dve.wait_ge(acc_zero, 1)

            def one_hot(i, u):
                rel = rel_cols[:, bass.ds(i, 1), u, :].rearrange("p a j -> p (a j)")
                dve.tensor_tensor(onehot[u][:, :, :],
                                  iota[:, 0:WIN].unsqueeze(1).broadcast_to([P, J, WIN]),
                                  rel.unsqueeze(2).broadcast_to([P, J, WIN]), ALU.is_equal).then_inc(onehot_ready, 1)

            def message(u, n):
                dve.wait_ge(multiplied, n + 1)
                dve.tensor_tensor(msg[SLOT[u]][:, :, :], ps_m[SLOT[u]][:, :].rearrange("p (j f) -> p j f", j=J),
                                  b_neg[:, :].unsqueeze(1).broadcast_to([P, J, F]), ALU.max).then_inc(msg_ready, 1)

            def add_window(u, n):
                base = dve.value_load(base_ok[0:1, bass.ds(n, 1)], min_val=0, max_val=N - 1)
                z, deg = acc[:, 0, bass.ds(base, WIN)], acc[:, 1, bass.ds(base, WIN)]
                if not isinstance(n, int) or n > 0:
                    dve.wait_ge(added, n)
                    dve.wait_ge(deg_added, n)
                dve.wait_ge(onehot_ready, n + 1)
                dve.tensor_reduce(deg_win[:, :], onehot[u][:, :, :].rearrange("p j w -> p w j"), AX.X, ALU.add
                                  ).then_inc(deg_summed, 1)
                dve.wait_ge(summed, n + 1)
                dve.tensor_tensor(z, z, ps_w[:, 0:WIN], ALU.add).then_inc(added, 1)
                dve.wait_ge(deg_summed, n + 1)
                dve.tensor_tensor(deg, deg, deg_win[:, :], ALU.add).then_inc(deg_added, 1)

            def finish(k, p):
                dve.wait_ge(part_in, 32 * k + 32)
                dve.tensor_tensor(xh[0:p, :, :], x_part[0:p, :, :], h_part[0:p, :, :], ALU.add).then_inc(xh_made, 1)
                dve.wait_ge(projected, k + 1)
                o = ps_f[0:p, 0:2 * C].rearrange("p (s c) -> p s c", s=2)
                dve.tensor_scalar(deg_max[0:p, :], o[:, :, D], 1.0, None, ALU.max).then_inc(f_max, 1)
                dve.wait_ge(f_max, k + 1)
                dve.reciprocal(deg_inv[0:p, :], deg_max[0:p, :]).then_inc(f_inv, 1)
                dve.wait_ge(f_inv, k + 1)
                dve.scalar_tensor_tensor(out=upd[0:p, :, :], in0=o[:, :, 0:D], scalar=0.0,
                                         in1=deg_inv[0:p, :].unsqueeze(2).broadcast_to([p, 2, D]),
                                         op0=ALU.max, op1=ALU.mult).then_inc(upd_made, 1)
                dve.wait_ge(xh_made, k + 1)
                dve.wait_ge(upd_made, k + 1)
                dve.tensor_tensor(res[0:p, :, :], upd[0:p, :, :], xh[0:p, :, :], ALU.add).then_inc(res_ready, 1)

            for u in range(U):
                one_hot(0, u)
                if u >= 1:
                    message(u - 1, u - 1)
                if u >= 2:
                    add_window(u - 2, u - 2)

            def loop_step(i, finishes):
                for u in range(U):
                    n = i * U + u
                    one_hot(i, u)
                    message((u - 1) % U, n - 1)
                    add_window((u - 2) % U, n - 2)
                    if u == 4 and finishes:
                        finish(i - LAG, FP)

            with dve.Fori(1, LAG) as i:
                loop_step(i, False)
            with dve.Fori(LAG, STEPS) as i:
                loop_step(i, True)

            message(U - 1, CHUNKS - 1)
            add_window(U - 2, CHUNKS - 2)
            dve.wait_ge(multiplied, DONE)
            dve.tensor_tensor(msg[SLOT[0]][0:TAIL, 0, :], ps_m[SLOT[0]][0:TAIL, 0:F], b_neg[0:TAIL, :], ALU.max
                              ).then_inc(msg_ready, 1)
            add_window(U - 1, CHUNKS - 1)
            base = dve.value_load(base_ok[0:1, CHUNKS:CHUNKS + 1], min_val=0, max_val=N - 1)
            dve.wait_ge(summed, DONE)
            dve.wait_ge(added, CHUNKS)
            dve.wait_ge(deg_added, CHUNKS)
            z, deg = acc[:, 0, bass.ds(base, WIN)], acc[0:TAIL, 1, bass.ds(base, WIN)]
            dve.tensor_tensor(z, z, ps_w[:, 0:WIN], ALU.add).then_inc(added, 1)
            dve.tensor_tensor(deg, deg, tail_onehot[:, :], ALU.add).then_inc(deg_added, 1)

            dve.wait_ge(added, DONE)
            dve.wait_ge(deg_added, DONE)
            for k in range(LOOP_FIN, LOOP_FIN + EXTRA):
                finish(k, NP)
            flag = dve.value_load(n_outside[0:1, 0:1], min_val=0, max_val=FLAG_MAX)
            with dve.If(flag > 0):
                dve.memset(acc[:, :, :], 0.0).then_inc(g_next, 1)
                dve.wait_ge(g_next, 1)
                with dve.Fori(0, GT) as t:
                    dve.wait_ge(g_in, 48 * t + 48)
                    dve.tensor_copy(g_dst_f[:, :], g_dst[:, :]).then_inc(g_dst_ready, 1)
                    dve.wait_ge(g_mult, t + 1)
                    dve.tensor_tensor(msg[0][0:GE, 0, :], ps_m[0][0:GE, 0:F], b_neg[0:GE, :], ALU.max).then_inc(g_msg, 1)
                    with dve.Fori(0, GB) as b:
                        m = t * GB + b
                        dve.wait_ge(g_dst_ready, m + t + 1)
                        dve.tensor_scalar(g_onehot, iota[0:GE, :], g_dst_f[:, 0:1], None, ALU.is_equal).then_inc(g_hot, 1)
                        dve.wait_ge(g_hot, m + 1)
                        dve.tensor_scalar(g_dst_f[:, :], g_dst_f[:, :], float(GN), None, ALU.subtract).then_inc(g_dst_ready, 1)
                        z, deg = acc[:, 0, bass.ds(b * GN, GN)], acc[0:GE, 1, bass.ds(b * GN, GN)]
                        dve.tensor_tensor(deg, deg, g_onehot, ALU.add).then_inc(g_added, 1)
                        dve.wait_ge(g_summed, m + 1)
                        dve.tensor_tensor(z, z, ps_g[:, 0:GN], ALU.add).then_inc(g_added, 1)
                        dve.wait_ge(g_added, 2 * m + 2)
                    dve.sem_inc(g_next, 1)
                dve.sem_inc(g_acc_done, 1)
                with dve.Fori(0, G_FIN) as b:
                    finish(b + (LOOP_FIN + EXTRA), NP)
            with dve.Else():
                dve.nop()


_INS = ['x', 'src', 'dst', 'edge_attr_64', 'L0_gnn_W_pre', 'L0_gnn_b_pre', 'L0_gnn_W_up', 'L0_gnn_b_up']
_OUTS = [((12500, 64), 'float32')]


def kernel(**inputs):
    import numpy as _np
    import concourse.bacc as _bacc
    from concourse import mybir as _mybir
    from concourse.bass_utils import run_bass_kernel_spmd as _run

    nc = _bacc.Bacc("TRN2", target_bir_lowering=False, num_devices=1)
    arrays, args = {}, []
    for name in _INS:
        a = _np.ascontiguousarray(inputs[name])
        arrays[f"in_{name}_dram"] = a
        args.append(nc.dram_tensor(f"in_{name}_dram", a.shape, _mybir.dt.from_np(a.dtype), kind="ExternalInput").ap())
    for i, (shape, dtype) in enumerate(_OUTS):
        dt = _mybir.dt.from_np(_np.dtype(dtype))
        args.append(nc.dram_tensor(f"out_{i}_dram", shape, dt, kind="ExternalOutput").ap())
    gnn_kernel(nc, *args)
    r = _run(nc, [arrays], core_ids=[0])
    return r.results[0]["out_0_dram"]
```

```python
import concourse.bass as bass
from concourse import mybir
from contextlib import ExitStack



def gnn_kernel(nc, x, src, dst, edge, W_pre, b_pre, W_up, b_up, out):
    f32, bf16, i32 = mybir.dt.float32, mybir.dt.bfloat16, mybir.dt.int32
    ALU, ACT, AX = mybir.AluOpType, mybir.ActivationFunctionType, mybir.AxisListType

    N, D = x.shape
    E, DE = edge.shape
    F = D + DE
    P = 128
    EPS = 1e-5

    J = 4
    CHUNK = J * P
    CHUNKS = E // CHUNK
    U = 5
    STEPS = CHUNKS // U
    TAIL0 = CHUNKS * CHUNK
    TAIL = E - TAIL0
    WIN = 64
    assert STEPS * U == CHUNKS and STEPS <= P and 0 < TAIL <= P and F == P

    NP = 125
    NK = N // NP
    PIECES = 4
    KA = [22, 22, 22, 14]
    KP = NK // PIECES
    assert NP * NK == N and PIECES * KP == NK

    GE = 125
    GT = E // GE
    GN = 500
    GB = -(-N // GN)
    assert GE * GT == E
    ACCW = max(GB * GN, N + WIN)

    FP = 75
    FIN = 2 * FP
    LAG = 3
    LOOP_FIN = STEPS - LAG
    HEAD = 1280
    ZERO_PAST = HEAD + 4096
    ZERO0 = 7
    ZEROINGS = [(row, first + k * (ACCW - first) // parts, first + (k + 1) * (ACCW - first) // parts)
                for row, first, parts in ((0, HEAD, 5), (1, ZERO_PAST, 3)) for k in range(parts)]
    assert ZERO0 + len(ZEROINGS) <= LAG * U
    MIDDLE = STEPS // 2
    EXTRA = (N - LOOP_FIN * FIN) // (2 * NP)
    G_FIN = N // (2 * NP)
    assert LOOP_FIN * FIN + EXTRA * 2 * NP == N and G_FIN * 2 * NP == N
    RAW = LAG
    BATCHES = [(n, min(n + 2, RAW * U)) for n in range(0, RAW * U, 2)]
    C = D + 1

    src_steps = src[0:TAIL0].rearrange("(i e) -> i e", i=STEPS)
    dst_steps = dst[0:TAIL0].rearrange("(i e) -> i e", i=STEPS)
    edge_chunks = edge[0:TAIL0, :].rearrange("(c p j) f -> c p j f", p=P, j=J)
    x_nodes = x.rearrange("(p k) f -> p k f", k=NK)

    h_table = nc.dram_tensor("h_table", [N, D], f32)
    h_table_nodes = h_table.rearrange("(p k) f -> p k f", k=NK)

    with ExitStack() as ctx:
        def sb(name, shape, dt=f32):
            return ctx.enter_context(nc.sbuf_tensor(name, shape, dt))

        def sem(name):
            return ctx.enter_context(nc.semaphore(name))

        ident = sb("ident", [P, P])
        ones = sb("ones", [P, 1])
        iota = sb("iota", [P, GN])
        eps, eps_root = sb("eps", [P, 1]), sb("eps_root", [P, 1])
        w_pre = sb("w_pre", [P, F])
        w_up = sb("w_up", [P, C])
        b_neg = sb("b_neg", [P, F])
        b_col = sb("b_col", [F, 1])
        b_wide = sb("b_wide", [F, P])
        b_up_all = sb("b_up_all", [P, D])
        b_last = sb("b_last", [P, C])

        x_area = sb("x_area", [P, NK * D])
        x_sb = x_area[0:NP, :].rearrange("p (k f) -> p k f", k=NK)
        stats = sb("stats", [NP, NK, 6])
        m_sum = sb("m_sum", [NP, NK])
        m_dif = sb("m_dif", [NP, NK])
        var = sb("var", [NP, NK])
        rstd = sb("rstd", [NP, NK])
        shift = sb("shift", [NP, NK])
        EROWS = RAW * U * J
        e_stats = sb("e_stats", [P, EROWS, 6])
        e_sum, e_dif, e_var, e_rstd = (sb(f"e_{name}", [P, EROWS]) for name in ("sum", "dif", "var", "rstd"))
        zeros = sb("zeros", [P, 1])
        h_nodes = sb("h_nodes", [NP, NK, D])
        base_f = sb("base_f", [STEPS, U])
        acc = sb("acc", [P, 2, ACCW])

        IDX = U * CHUNK
        src_f, dst_f = acc[0:STEPS, 0, HEAD:HEAD + IDX], acc[0:STEPS, 0, HEAD + IDX:HEAD + 2 * IDX]
        first_src = sb("first_src", [P, U, J], i32)
        src_cols = sb("src_cols", [P, STEPS + 1, U, J], i32)
        rel_cols = sb("rel_cols", [P, STEPS, U, J])
        base_row = sb("base_row", [1, CHUNKS + 1], i32)
        base_ok = sb("base_ok", [1, CHUNKS + 1], i32)
        base_min = sb("base_min", [1, STEPS], i32)
        misplaced = sb("misplaced", [1, CHUNKS + 1])
        n_misplaced = sb("n_misplaced", [1, 2])
        assert (CHUNKS + 1) % 2 == 0
        ext = sb("ext", [P, 2])
        outside = sb("outside", [P, 2])
        n_outside_f = sb("n_outside_f", [1, 1])
        n_outside = sb("n_outside", [1, 1], i32)

        comb = [sb(f"comb{u}", [P, J, F]) for u in range(U)]
        src_idx = [sb(f"src_idx{u}", [P, J], i32) for u in range(U)]
        onehot = [sb(f"onehot{u}", [P, J, WIN]) for u in range(U)]
        SLOT = [0, 1, 0, 1, 2]
        assert len(SLOT) == U
        comb_t = [sb(f"comb_t{b}", [F, J, P]) for b in range(3)]
        msg = [sb(f"msg{b}", [P, J, F]) for b in range(3)]
        deg_win = sb("deg_win", [P, WIN])

        tail_comb = sb("tail_comb", [TAIL, F])
        tail_src = sb("tail_src", [TAIL, 1], i32)
        tail_dst = sb("tail_dst", [TAIL, 2], i32)
        tail_dst_f = sb("tail_dst_f", [TAIL, 2])
        tail_rel = sb("tail_rel", [TAIL, 1])
        tail_out = sb("tail_out", [TAIL, 2])
        tail_onehot = sb("tail_onehot", [TAIL, WIN])

        g_dst = sb("g_dst", [GE, 1], i32)
        g_src = sb("g_src", [GE, 1], i32)
        g_dst_f = sb("g_dst_f", [GE, 1])
        g_onehot = comb[1][0:GE, :, :].rearrange("p j f -> p (j f)")[:, 0:GN]

        sums = x_area[:, 0:4 * NP].rearrange("q (c s p) -> q c s p", c=2, s=2)
        rows = [x_area[0:NP, 8 * NP + 2 * D * q:8 * NP + 2 * D * (q + 1)].rearrange("p (s f) -> p s f", s=2)
                for q in range(5 + 4 * EXTRA)]
        x_part, h_part, xh, upd, res = rows[0:5]
        assert EXTRA == 2
        more_sums = [sums, x_area[:, 4 * NP:8 * NP].rearrange("q (c s p) -> q c s p", c=2, s=2)]
        more_x, more_h, more_xh, more_res = (rows[5 + q * EXTRA:5 + (q + 1) * EXTRA] for q in range(4))
        deg_max = sb("deg_max", [NP, 2])
        deg_inv = sb("deg_inv", [NP, 2])

        bank = [ctx.enter_context(nc.psum_tensor(f"bank{i}", [P, 512], f32)) for i in range(8)]
        ps_t = bank[0:3]
        ps_m = bank[3:6]
        ps_w = bank[6]
        ps_cnt, ps_bias = bank[7], bank[7]
        ps_g = bank[6]
        ps_f = bank[7]
        more_ps = [bank[7], bank[1]]
        src_banks, dst_banks = bank[0:4], bank[4:8]

        x_in = [sem(f"x_in{g}") for g in range(PIECES)]
        first_src_in = sem("first_src_in")
        src_in, dst_in, base_in, tail_in, bias_in, weights_in = (
            sem("src_in"), sem("dst_in"), sem("base_in"), sem("tail_in"), sem("bias_in"), sem("weights_in"))
        consts_made, pool_prep, v_prep = sem("consts_made"), sem("pool_prep"), sem("v_prep")
        src_float, dst_rel = sem("src_float"), sem("dst_rel")
        src_turned, rel_turned = sem("src_turned"), sem("rel_turned")
        src_cols_done, rel_cols_done = sem("src_cols_done"), sem("rel_cols_done")
        var_done, std_done, scale_done = sem("var_done"), sem("std_done"), sem("scale_done")
        iota_wide = sem("iota_wide")
        h_by_act, h_by_dve, h_stored = sem("h_by_act"), sem("h_by_dve"), sem("h_stored")
        e_var_done, e_std_done, e_diff_done, e_ready = (
            sem("e_var_done"), sem("e_std_done"), sem("e_diff_done"), sem("e_ready"))
        acc_zero = sem("acc_zero")
        b_wide_made, bias_multiplied, bias_made = sem("b_wide_made"), sem("bias_multiplied"), sem("bias_made")
        out_cols, counted, flag_ready = sem("out_cols"), sem("counted"), sem("flag_ready")
        edge_in = [sem(f"edge_in{u}") for u in range(U)]
        h_in = [sem(f"h_in{u}") for u in range(U)]
        src_idx_set, gathers_begun = sem("src_idx_set"), sem("gathers_begun")
        turned, evacuated, multiplied = sem("turned"), sem("evacuated"), sem("multiplied")
        msg_ready, onehot_ready, summed, added = sem("msg_ready"), sem("onehot_ready"), sem("summed"), sem("added")
        deg_summed, deg_added = sem("deg_summed"), sem("deg_added")
        tail_h_in = sem("tail_h_in")
        g_in, g_h_in, g_turned, g_evac, g_mult = sem("g_in"), sem("g_h_in"), sem("g_turned"), sem("g_evac"), sem("g_mult")
        g_msg, g_hot, g_summed, g_added, g_dst_ready, g_next = (
            sem("g_msg"), sem("g_hot"), sem("g_summed"), sem("g_added"), sem("g_dst_ready"), sem("g_next"))
        part_in, more_in, staged, projected = sem("part_in"), sem("more_in"), sem("staged"), sem("projected")
        xh_made, f_max, f_inv, upd_made, res_ready, stored = (
            sem("xh_made"), sem("f_max"), sem("f_inv"), sem("upd_made"), sem("res_ready"), sem("stored"))
        g_acc_done = sem("g_acc_done")

        DONE = CHUNKS + 1
        FLAG_MAX = 2 * P + 2 * TAIL + CHUNKS + 1

        def nodes_of(tensor, first, p):
            return tensor[bass.ds(first, 2 * p), :].rearrange("(s p) f -> p s f", s=2)

        def after_loop(k):
            return LOOP_FIN * FIN + (k - LOOP_FIN) * 2 * NP

        def node_piece(g):
            return slice(g * KP, (g + 1) * KP)

        block = ctx.enter_context(nc.Block())

        @block.sync
        def _(sp):
            sp.dma_start(first_src[:, :, :], src[0:IDX].rearrange("(u p j) -> p u j", u=U, p=P)).then_inc(first_src_in, 16)

            def load_x(g):
                sp.dma_start(x_sb[:, node_piece(g), :], x_nodes[:, node_piece(g), :]).then_inc(x_in[g], 16)

            load_x(0)
            sp.dma_start(src_f.bitcast(i32), src_steps).then_inc(src_in, 16)
            with nc.allow_non_contiguous_dma(reason="one index of each chunk"):
                sp.dma_start(base_row[:, 0:CHUNKS],
                             dst[0:TAIL0].rearrange("(a c e) -> a c e", a=1, e=CHUNK)[:, :, 0]).then_inc(base_in, 16)
            sp.dma_start(base_row[:, CHUNKS:CHUNKS + 1], dst[TAIL0:TAIL0 + 1].rearrange("(a b) -> a b", a=1)
                         ).then_inc(base_in, 16)
            sp.dma_start(b_neg[:, :], b_pre.rearrange("(a f) -> a f", a=1).broadcast_to([P, F])).then_inc(bias_in, 16)
            load_x(1)
            sp.dma_start(w_pre[:, :], W_pre).then_inc(weights_in, 16)
            sp.dma_start(dst_f.bitcast(i32), dst_steps).then_inc(dst_in, 16)

            def load_edges(i, u):
                sp.dma_start(comb[u][:, :, D:F],
                             edge_chunks[bass.ds(i * U + u, 1), :, :, :].rearrange("c p j f -> (c p) j f")
                             ).then_inc(edge_in[u], 16)

            for u in range(2):
                load_edges(0, u)
            sp.wait_ge(h_in[1], 16 * J)
            for u in range(2, U):
                load_edges(0, u)
            sp.dma_start(w_up[:, 0:D], W_up).then_inc(weights_in, 16)
            sp.dma_start(b_up_all[:, :], b_up.rearrange("(a f) -> a f", a=1).broadcast_to([P, D])).then_inc(weights_in, 16)
            sp.dma_start(b_col[:, :], b_pre.rearrange("(f a) -> f a", a=1)).then_inc(weights_in, 16)
            sp.dma_start(tail_src[:, :], src[TAIL0:E].rearrange("(p a) -> p a", a=1)).then_inc(tail_in, 16)
            sp.dma_start(tail_dst[:, 0:1], dst[TAIL0:E].rearrange("(p a) -> p a", a=1)).then_inc(tail_in, 16)
            sp.dma_start(tail_dst[:, 1:2], dst[TAIL0:TAIL0 + 1].rearrange("(p a) -> p a", a=1).broadcast_to([TAIL, 1])
                         ).then_inc(tail_in, 16)
            sp.dma_start(tail_comb[:, D:F], edge[TAIL0:E, :]).then_inc(tail_in, 16)
            for g in range(2, PIECES):
                load_x(g)

            def load_next_edges(i, u):
                sp.wait_ge(turned, i * U + (u - U + 1))
                load_edges(i, u)

            for g in range(PIECES):
                sp.wait_ge(h_by_act, 2 * g + 2)
                sp.wait_ge(h_by_dve, g + 1)
                sp.dma_start(h_table_nodes[:, node_piece(g), :], h_nodes[:, node_piece(g), :]).then_inc(h_stored, 16)
                for u in {1: (0, 1), 2: (2, 3, 4)}.get(g, ()):
                    load_next_edges(1, u)

            def load_part(first, p):
                sp.dma_start(x_part[0:p, :, :], nodes_of(x, first, p)).then_inc(part_in, 16)
                sp.dma_start(h_part[0:p, :, :], nodes_of(h_table, first, p)).then_inc(part_in, 16)

            def store_result(k, first, p):
                sp.wait_ge(res_ready, k + 1)
                sp.dma_start(nodes_of(out, first, p), res[0:p, :, :]).then_inc(stored, 16)

            def loop_step(i, store, load):
                for u in range(U):
                    load_next_edges(i, u)
                    if u == 0 and store:
                        store_result(i - (LAG + 1), (i - (LAG + 1)) * FIN, FP)
                    if u == 2 and load:
                        if store:
                            sp.wait_ge(stored, 16 * (i - LAG))
                        load_part((i - LAG) * FIN, FP)

            for i in range(2, LAG):
                loop_step(i, False, False)
            loop_step(LAG, False, True)
            with sp.Fori(LAG + 1, STEPS) as i:
                loop_step(i, True, True)
            for e in range(EXTRA):
                first = after_loop(LOOP_FIN + e)
                sp.dma_start(more_x[e], nodes_of(x, first, NP)).then_inc(more_in, 16)
                sp.dma_start(more_h[e], nodes_of(h_table, first, NP)).then_inc(more_in, 16)
            last = LOOP_FIN - 1
            store_result(last, last * FIN, FP)
            for e in range(EXTRA):
                k = LOOP_FIN + e
                sp.wait_ge(res_ready, k + 1)
                sp.dma_start(nodes_of(out, after_loop(k), NP), more_res[e]).then_inc(stored, 16)

            flag = sp.value_load(n_outside[0:1, 0:1], min_val=0, max_val=FLAG_MAX)
            sp.wait_ge(stored, 16 * (LOOP_FIN + EXTRA))
            with sp.If(flag > 0):
                with sp.Fori(0, GT) as t:
                    sp.wait_ge(g_next, t + 1)
                    sp.dma_start(g_dst[:, :], dst[bass.ds(t * GE, GE)].rearrange("(p a) -> p a", a=1)).then_inc(g_in, 16)
                    sp.dma_start(g_src[:, :], src[bass.ds(t * GE, GE)].rearrange("(p a) -> p a", a=1)).then_inc(g_in, 16)
                    sp.dma_start(comb[0][0:GE, 0, D:F], edge[bass.ds(t * GE, GE), :]).then_inc(g_in, 16)
                with sp.Fori(0, G_FIN) as b:
                    sp.wait_ge(stored, 16 * b + 16 * (LOOP_FIN + EXTRA))
                    load_part(b * 2 * NP, NP)
                    store_result(b + (LOOP_FIN + EXTRA), b * 2 * NP, NP)
                sp.wait_ge(stored, 16 * (LOOP_FIN + EXTRA + G_FIN))
            with sp.Else():
                sp.nop()

        @block.gpsimd
        def _(pool):
            steps = [0]

            def step(ins):
                steps[0] += 1
                ins.then_inc(pool_prep, 1)
                pool.wait_ge(pool_prep, steps[0])

            step(pool.memset(ident[:, :], 0.0))
            pool.affine_select(out=ident[:, :], in_=ident[:, :], compare_op=ALU.not_equal, fill=1.0,
                               base=0, pattern=[[-1, P]], channel_multiplier=1).then_inc(consts_made, 1)
            pool.iota(iota[:, 0:WIN], pattern=[[1, WIN]], base=0, channel_multiplier=0,
                      allow_small_or_imprecise_dtypes=True).then_inc(consts_made, 1)
            pool.iota(base_min[:, :], pattern=[[FIN, STEPS]], base=-(LAG - 1) * FIN, channel_multiplier=0
                      ).then_inc(consts_made, 1)

            def gather(u, table, index):
                pool.sem_inc(gathers_begun, 1)
                for j in range(J):
                    pool.indirect_dma_start(
                        out=comb[u][:, j, 0:D], out_offset=None, in_=table[:, :],
                        in_offset=bass.IndirectOffsetOnAxis(ap=index[:, j:j + 1], axis=0),
                        bounds_check=N - 1).then_inc(h_in[u], 16)

            pool.wait_ge(first_src_in, 16)
            for u in range(U):
                gather(u, x, first_src[:, u, :])
            pool.wait_ge(src_cols_done, 4 + 1)
            for i in range(1, RAW):
                for u in range(U):
                    pool.wait_ge(turned, i * U + (u - U + 1))
                    gather(u, x, src_cols[:, i, u, :])
            pool.wait_ge(h_stored, 16 * PIECES)
            with pool.Fori(RAW, STEPS) as i:
                for u in range(U):
                    pool.wait_ge(src_idx_set, i * U + (u - RAW * U + 1))
                    pool.wait_ge(turned, i * U + (u - U + 1))
                    gather(u, h_table, src_idx[u])
            pool.wait_ge(tail_in, 16 * 4)
            pool.indirect_dma_start(
                out=tail_comb[:, 0:D], out_offset=None, in_=h_table[:, :],
                in_offset=bass.IndirectOffsetOnAxis(ap=tail_src[:, 0:1], axis=0),
                bounds_check=N - 1).then_inc(tail_h_in, 16)

            pool.wait_ge(flag_ready, 1)
            flag = pool.value_load(n_outside[0:1, 0:1], min_val=0, max_val=FLAG_MAX)
            with pool.If(flag > 0):
                pool.wait_ge(onehot_ready, CHUNKS)
                pool.iota(iota[:, :], pattern=[[1, GN]], base=0, channel_multiplier=0,
                          allow_small_or_imprecise_dtypes=True).then_inc(iota_wide, 1)
                with pool.Fori(0, GT) as t:
                    pool.wait_ge(g_in, 48 * t + 48)
                    pool.sem_inc(gathers_begun, 1)
                    pool.indirect_dma_start(
                        out=comb[0][0:GE, 0, 0:D], out_offset=None, in_=h_table[:, :],
                        in_offset=bass.IndirectOffsetOnAxis(ap=g_src[:, 0:1], axis=0),
                        bounds_check=N - 1).then_inc(g_h_in, 16)
            with pool.Else():
                pool.nop()

        @block.scalar
        def _(act):
            act.wait_ge(v_prep, 1)
            act.activation(eps_root[:, :], eps[:, :], ACT.Sqrt)

            def clear(row, first, past):
                act.activation(acc[:, row, first:past], zeros[:, 0:1].broadcast_to([P, past - first]), ACT.Copy
                               ).then_inc(acc_zero, 1)

            def root(g):
                ks = node_piece(g)
                act.wait_ge(var_done, g + 1)
                act.activation(rstd[:, ks], var[:, ks], ACT.Sqrt, scale=1.0 / D, bias=eps[0:NP, 0:1]).then_inc(std_done, 1)

            def normalize(g, half):
                act.wait_ge(scale_done, g + 1)
                for k in range(g * KP + half * (KA[g] // 2), g * KP + (KA[g] // 2, KA[g])[half]):
                    last = act.activation(h_nodes[:, k, :], x_sb[:, k, :], ACT.Relu,
                                          scale=rstd[:, k:k + 1], bias=shift[:, k:k + 1])
                last.then_inc(h_by_act, 1)

            def batch_root(b):
                rows = slice(BATCHES[b][0] * J, BATCHES[b][1] * J)
                act.wait_ge(e_var_done, b + 1)
                act.activation(e_rstd[:, rows], e_var[:, rows], ACT.Sqrt, scale=1.0 / D, bias=eps[:, 0:1]
                               ).then_inc(e_std_done, 1)

            clear(1, HEAD, ZERO_PAST)
            root(0)
            act.wait_ge(src_in, 16)
            act.activation(src_f, src_f.bitcast(i32), ACT.Copy).then_inc(src_float, 1)
            normalize(0, 0)
            root(1)
            per_bank = U * J // 4
            src_flat = src_cols[:, 0:STEPS, :, :].rearrange("p i u j -> p i (u j)")
            for q in range(4):
                act.wait_ge(src_turned, q + 1)
                act.activation(src_flat[:, :, q * per_bank:(q + 1) * per_bank],
                               src_banks[q][:, 0:per_bank * STEPS].rearrange("p (m i) -> p i m", m=per_bank),
                               ACT.Copy).then_inc(src_cols_done, 1)
            act.wait_ge(src_cols_done, 4 + 1)
            for u in range(U):
                act.activation(src_idx[u][:, :], src_cols[:, RAW, u, :], ACT.Copy).then_inc(src_idx_set, 1)
            batch_root(0)
            normalize(0, 1)
            normalize(1, 0)
            batch_root(1)

            def chunk(i, u):
                n = i * U + u
                act.wait_ge(turned, n + 1)
                if not isinstance(i, int):
                    act.activation(src_idx[u][:, :], src_cols[:, bass.ds(i + 1, 1), u, :].rearrange("p a j -> p (a j)"),
                                   ACT.Copy).then_inc(src_idx_set, 1)
                if not isinstance(i, int) or u >= 2:
                    act.wait_ge(multiplied, n - 1)
                act.activation(comb_t[SLOT[u]][:, :, :], ps_t[SLOT[u]][:, :].rearrange("p (j e) -> p j e", j=J), ACT.Copy
                               ).then_inc(evacuated, 1)

            def stage(first, p, sums=sums):
                nodes = acc[:, :, bass.ds(first, 2 * p)].rearrange("q c (s p) -> q c s p", s=2)
                act.activation(sums[:, :, :, 0:p], nodes, ACT.Copy).then_inc(staged, 1)

            for i in range(LAG):
                for u in range(U):
                    chunk(i, u)
                    n = i * U + u
                    if n == 0:
                        normalize(1, 1)
                    if n == 1:
                        batch_root(2)
                    if n == 3:
                        root(2)
                        normalize(2, 0)
                        batch_root(3)
                    if n == 4:
                        normalize(2, 1)
                    if n == 5:
                        root(3)
                        normalize(3, 0)
                    if n == 6:
                        normalize(3, 1)
                    if n >= 6 and n % 2 == 0 and n // 2 + 1 < len(BATCHES):
                        batch_root(n // 2 + 1)
                    if 0 <= n - ZERO0 < len(ZEROINGS):
                        clear(*ZEROINGS[n - ZERO0])
            act.wait_ge(acc_zero, 2 + len(ZEROINGS))
            with act.Fori(LAG, STEPS) as i:
                for u in range(U):
                    chunk(i, u)
                    if u == 2:
                        act.wait_ge(added, i * U)
                        act.wait_ge(deg_added, i * U)
                        stage((i - LAG) * FIN, FP)
            act.wait_ge(turned, DONE)
            act.activation(comb_t[SLOT[0]][:, 0, 0:TAIL], ps_t[SLOT[0]][:, 0:TAIL], ACT.Copy).then_inc(evacuated, 1)

            act.wait_ge(added, DONE)
            act.wait_ge(deg_added, DONE)
            act.wait_ge(projected, LOOP_FIN)
            for e in range(EXTRA):
                stage(after_loop(LOOP_FIN + e), NP, more_sums[e])

            flag = act.value_load(n_outside[0:1, 0:1], min_val=0, max_val=FLAG_MAX)
            with act.If(flag > 0):
                with act.Fori(0, GT) as t:
                    act.wait_ge(g_turned, t + 1)
                    act.activation(comb_t[0][:, 0, 0:GE], ps_t[0][:, 0:GE], ACT.Copy).then_inc(g_evac, 1)
                with act.Fori(0, G_FIN) as b:
                    act.wait_ge(g_acc_done, 1)
                    act.wait_ge(projected, b + (LOOP_FIN + EXTRA))
                    stage(b * 2 * NP, NP)
            with act.Else():
                act.nop()

        @block.tensor
        def _(pe):
            pe.wait_ge(consts_made, 3)

            def turn_indices(values, banks, done):
                per_bank = U * J // 4
                for q in range(4):
                    for m in range(per_bank):
                        u, j = divmod(q * per_bank + m, J)
                        last = pe.transpose(banks[q][:, m * STEPS:(m + 1) * STEPS],
                                            values[:, u * CHUNK + j:(u + 1) * CHUNK:J], ident[0:STEPS, 0:STEPS])
                    last.then_inc(done, 1)

            pe.wait_ge(src_float, 1)
            turn_indices(src_f, src_banks, src_turned)
            pe.wait_ge(src_cols_done, 4 + 1)
            def turn(i, u):
                pe.wait_ge(edge_in[u], 16 * i + 16)
                pe.wait_ge(h_in[u], 16 * J * i + 16 * J)
                for j in range(J):
                    last = pe.transpose(ps_t[SLOT[u]][:, j * P:(j + 1) * P], comb[u][:, j, :], ident[:, :])
                last.then_inc(turned, 1)

            def multiply(u, n):
                pe.wait_ge(evacuated, n + 1)
                for j in range(J):
                    last = pe.matmul(ps_m[SLOT[u]][:, j * F:(j + 1) * F], comb_t[SLOT[u]][:, j, :], w_pre[:, :],
                                     start=True, stop=True)
                last.then_inc(multiplied, 1)

            def sum_window(u, n, first):
                pe.wait_ge(msg_ready, n + 1)
                pe.wait_ge(onehot_ready, n + 1)
                if not first:
                    pe.wait_ge(added, n)
                for j in range(J):
                    last = pe.matmul(ps_w[:, 0:WIN], msg[SLOT[u]][:, j, :], onehot[u][:, j, :],
                                     start=(j == 0), stop=(j == J - 1))
                last.then_inc(summed, 1)

            def project(p, sums=sums, ps=ps_f):
                for q in range(2):
                    o = ps[0:p, q * C:(q + 1) * C]
                    pe.matmul(o, sums[:, 0, q, 0:p], w_up[:, :], start=True, stop=False)
                    last = pe.matmul(o, sums[:, 1, q, 0:p], b_last[:, :], start=False, stop=True)
                last.then_inc(projected, 1)

            def loop_step(i):
                for u in range(U):
                    n = i * U + u
                    turn(i, u)
                    multiply((u - 1) % U, n - 1)
                    sum_window((u - 2) % U, n - 2, False)
                    if u == 3:
                        pe.wait_ge(staged, i - (LAG - 1))
                        project(FP)

            for i in range(LAG):
                for u in range(U):
                    n = i * U + u
                    for b, (first, past) in enumerate(BATCHES):
                        if first <= n < past:
                            pe.wait_ge(e_ready, b + 1)
                    turn(i, u)
                    if n == 1:
                        pe.wait_ge(dst_rel, U)
                        turn_indices(dst_f, dst_banks, rel_turned)
                        pe.wait_ge(weights_in, 16 * 4)
                    if n == 2:
                        pe.wait_ge(rel_cols_done, 4)
                    if n >= 1:
                        multiply((u - 1) % U, n - 1)
                    if n >= 2:
                        sum_window((u - 2) % U, n - 2, n == 2)
                    if n == U + 1:
                        pe.wait_ge(b_wide_made, 1)
                        pe.matmul(ps_bias[:, 0:D], b_wide[:, :], w_up[:, 0:D], start=True, stop=True
                                  ).then_inc(bias_multiplied, 1)
            pe.wait_ge(bias_made, 1)
            with pe.Fori(LAG, MIDDLE) as i:
                loop_step(i)
            pe.wait_ge(out_cols, 1)
            pe.matmul(ps_cnt[0:1, 0:2], ones[:, 0:1], outside[:, :], start=True, stop=False)
            pe.matmul(ps_cnt[0:1, 0:2], ones[0:TAIL, 0:1], tail_out[:, :], start=False, stop=False)
            pe.matmul(ps_cnt[0:1, 0:2], ones[0:1, 0:1], n_misplaced[:, :], start=False, stop=True).then_inc(counted, 1)
            pe.wait_ge(flag_ready, 1)
            with pe.Fori(MIDDLE, STEPS) as i:
                loop_step(i)

            pe.wait_ge(tail_in, 16 * 4)
            pe.wait_ge(tail_h_in, 16)
            pe.transpose(ps_t[SLOT[0]][:, 0:TAIL], tail_comb[:, :], ident[0:TAIL, 0:TAIL]).then_inc(turned, 1)
            multiply(U - 1, CHUNKS - 1)
            sum_window(U - 2, CHUNKS - 2, False)
            pe.wait_ge(evacuated, DONE)
            pe.matmul(ps_m[SLOT[0]][0:TAIL, 0:F], comb_t[SLOT[0]][:, 0, 0:TAIL], w_pre[:, :], start=True, stop=True
                      ).then_inc(multiplied, 1)
            sum_window(U - 1, CHUNKS - 1, False)
            pe.wait_ge(msg_ready, DONE)
            pe.wait_ge(added, CHUNKS)
            pe.matmul(ps_w[:, 0:WIN], msg[SLOT[0]][0:TAIL, 0, :], tail_onehot[:, :], start=True, stop=True
                      ).then_inc(summed, 1)

            pe.wait_ge(upd_made, LOOP_FIN)
            for e in range(EXTRA):
                pe.wait_ge(staged, LOOP_FIN + e + 1)
                project(NP, more_sums[e], more_ps[e])

            flag = pe.value_load(n_outside[0:1, 0:1], min_val=0, max_val=FLAG_MAX)
            with pe.If(flag > 0):
                with pe.Fori(0, GT) as t:
                    pe.wait_ge(g_in, 48 * t + 48)
                    pe.wait_ge(g_h_in, 16 * t + 16)
                    pe.transpose(ps_t[0][:, 0:GE], comb[0][0:GE, 0, :], ident[0:GE, 0:GE]).then_inc(g_turned, 1)
                    pe.wait_ge(g_evac, t + 1)
                    pe.matmul(ps_m[0][0:GE, 0:F], comb_t[0][:, 0, 0:GE], w_pre[:, :], start=True, stop=True
                              ).then_inc(g_mult, 1)
                    with pe.Fori(0, GB) as b:
                        pe.wait_ge(g_msg, t + 1)
                        pe.wait_ge(g_hot, t * GB + b + 1)
                        pe.matmul(ps_g[:, 0:GN], msg[0][0:GE, 0, :], g_onehot, start=True, stop=True).then_inc(g_summed, 1)
                with pe.Fori(0, G_FIN) as b:
                    pe.wait_ge(staged, b + (LOOP_FIN + EXTRA + 1))
                    pe.wait_ge(upd_made, b + (LOOP_FIN + EXTRA))
                    project(NP)
            with pe.Else():
                pe.nop()

        @block.vector
        def _(dve):
            steps = [0]

            def step(ins):
                steps[0] += 1
                ins.then_inc(v_prep, 1)
                dve.wait_ge(v_prep, steps[0])

            dve.memset(w_up[:, D:C], 0.0)
            dve.memset(b_last[:, D:C], 1.0)
            dve.memset(ones[:, :], 1.0)
            dve.memset(src_cols[:, STEPS, :, :], 0).then_inc(src_cols_done, 1)
            dve.memset(zeros[:, :], 0.0)
            step(dve.memset(eps[:, :], EPS))

            dve.memset(acc[:, :, 0:HEAD], 0.0).then_inc(acc_zero, 1)

            def statistics(rows, st, total, dif, v, done):
                for k, row in enumerate(rows):
                    last = dve.bn_stats(st[:, k, :], row)
                step(last)
                dve.tensor_tensor(total, st[:, :, 1], st[:, :, 4], ALU.add)
                dve.tensor_tensor(dif, st[:, :, 1], st[:, :, 4], ALU.subtract)
                step(dve.tensor_tensor(v, st[:, :, 2], st[:, :, 5], ALU.add))
                step(dve.tensor_tensor(dif, dif, dif, ALU.mult))
                dve.scalar_tensor_tensor(out=v, in0=dif, scalar=D / 4.0, in1=v,
                                         op0=ALU.mult, op1=ALU.add).then_inc(done, 1)

            def less_mean(o, rows, total):
                return dve.scalar_tensor_tensor(out=o, in0=total.unsqueeze(2).broadcast_to(list(o.shape)), scalar=-0.5, in1=rows,
                                                op0=ALU.mult, op1=ALU.add)

            def scale_relu(rows, r):
                return dve.scalar_tensor_tensor(out=rows, in0=rows, scalar=0.0,
                                                in1=r.unsqueeze(2).broadcast_to(list(rows.shape)),
                                                op0=ALU.max, op1=ALU.mult)

            def node_statistics(g):
                ks = node_piece(g)
                dve.wait_ge(x_in[g], 16)
                statistics([x_sb[:, k, :] for k in range(g * KP, (g + 1) * KP)],
                           stats[:, ks, :], m_sum[:, ks], m_dif[:, ks], var[:, ks], var_done)

            def normalize(g):
                theirs, mine = slice(g * KP, g * KP + KA[g]), slice(g * KP + KA[g], (g + 1) * KP)
                dve.wait_ge(std_done, g + 1)
                step(dve.reciprocal(rstd[:, node_piece(g)], rstd[:, node_piece(g)]))
                dve.scalar_tensor_tensor(out=shift[:, theirs], in0=m_sum[:, theirs], scalar=-0.5, in1=rstd[:, theirs],
                                         op0=ALU.mult, op1=ALU.mult).then_inc(scale_done, 1)
                step(less_mean(h_nodes[:, mine, :], x_sb[:, mine, :], m_sum[:, mine]))
                scale_relu(h_nodes[:, mine, :], rstd[:, mine]).then_inc(h_by_dve, 1)

            def batch_statistics(b):
                first, past = BATCHES[b]
                ts = slice(first * J, past * J)
                for n in range(first, past):
                    dve.wait_ge(h_in[n % U], 16 * J * (n // U + 1))
                statistics([comb[n % U][:, j, 0:D] for n in range(first, past) for j in range(J)],
                           e_stats[:, ts, :], e_sum[:, ts], e_dif[:, ts], e_var[:, ts], e_var_done)
                for n in range(first, past):
                    own = comb[n % U][:, :, 0:D]
                    last = less_mean(own, own, e_sum[:, n * J:(n + 1) * J])
                last.then_inc(e_diff_done, 1)

            def batch_normalize(b):
                first, past = BATCHES[b]
                ts = slice(first * J, past * J)
                dve.wait_ge(e_std_done, b + 1)
                step(dve.reciprocal(e_rstd[:, ts], e_rstd[:, ts]))
                dve.wait_ge(e_diff_done, b + 1)
                for n in range(first, past):
                    last = scale_relu(comb[n % U][:, :, 0:D], e_rstd[:, n * J:(n + 1) * J])
                last.then_inc(e_ready, 1)

            node_statistics(0)
            normalize(0)
            node_statistics(1)
            batch_statistics(0)
            normalize(1)
            batch_normalize(0)
            dve.wait_ge(consts_made, 3)
            dve.wait_ge(base_in, 32)
            step(dve.tensor_tensor(base_ok[:, 0:CHUNKS].rearrange("a (i u) -> a i u", u=U),
                                   base_row[:, 0:CHUNKS].rearrange("a (i u) -> a i u", u=U),
                                   base_min[:, :].unsqueeze(2).broadcast_to([1, STEPS, U]), ALU.max))
            dve.tensor_scalar(base_ok[:, CHUNKS:CHUNKS + 1], base_row[:, CHUNKS:CHUNKS + 1],
                              float(LOOP_FIN * FIN), float(N - 1), ALU.max, ALU.min)
            dve.tensor_scalar(base_ok[:, LAG * U:CHUNKS], base_ok[:, LAG * U:CHUNKS], 0.0, float(N - 1), ALU.max, ALU.min)
            step(dve.tensor_scalar(base_ok[:, 0:LAG * U], base_ok[:, 0:LAG * U], 0.0, float(HEAD - WIN), ALU.max, ALU.min))
            dve.wait_ge(bias_in, 16)
            step(dve.tensor_scalar(b_neg[:, :], b_neg[:, :], -1.0, None, ALU.mult))
            dve.wait_ge(dst_in, 16)
            step(dve.tensor_copy(base_f[:, :], dst_f.bitcast(i32).rearrange("i (u e) -> i u e", u=U)[:, :, 0]))
            for u in range(U):
                part = dst_f[:, u * CHUNK:(u + 1) * CHUNK]
                dve.tensor_scalar(part, part.bitcast(i32), base_f[:, u:u + 1], None, ALU.subtract).then_inc(dst_rel, 1)
            batch_statistics(1)
            per_bank = U * J // 4
            rel_flat = rel_cols[:, :, :, :].rearrange("p i u j -> p i (u j)")
            for q in range(4):
                dve.wait_ge(rel_turned, q + 1)
                dve.tensor_copy(rel_flat[:, :, q * per_bank:(q + 1) * per_bank],
                                dst_banks[q][:, 0:per_bank * STEPS].rearrange("p (m i) -> p i m", m=per_bank)
                                ).then_inc(rel_cols_done, 1)
            batch_normalize(1)
            dve.wait_ge(rel_cols_done, 4)

            def one_hot(i, u):
                rel = rel_cols[:, bass.ds(i, 1), u, :].rearrange("p a j -> p (a j)")
                dve.tensor_tensor(onehot[u][:, :, :],
                                  iota[:, 0:WIN].unsqueeze(1).broadcast_to([P, J, WIN]),
                                  rel.unsqueeze(2).broadcast_to([P, J, WIN]), ALU.is_equal).then_inc(onehot_ready, 1)

            def message(u, n):
                dve.wait_ge(multiplied, n + 1)
                dve.tensor_tensor(msg[SLOT[u]][:, :, :], ps_m[SLOT[u]][:, :].rearrange("p (j f) -> p j f", j=J),
                                  b_neg[:, :].unsqueeze(1).broadcast_to([P, J, F]), ALU.max).then_inc(msg_ready, 1)

            def add_window(u, n):
                base = dve.value_load(base_ok[0:1, bass.ds(n, 1)], min_val=0, max_val=N - 1)
                z, deg = acc[:, 0, bass.ds(base, WIN)], acc[:, 1, bass.ds(base, WIN)]
                if not isinstance(n, int) or n > 0:
                    dve.wait_ge(added, n)
                    dve.wait_ge(deg_added, n)
                dve.wait_ge(onehot_ready, n + 1)
                dve.tensor_reduce(deg_win[:, :], onehot[u][:, :, :].rearrange("p j w -> p w j"), AX.X, ALU.add
                                  ).then_inc(deg_summed, 1)
                dve.wait_ge(summed, n + 1)
                dve.tensor_tensor(z, z, ps_w[:, 0:WIN], ALU.add).then_inc(added, 1)
                dve.wait_ge(deg_summed, n + 1)
                dve.tensor_tensor(deg, deg, deg_win[:, :], ALU.add).then_inc(deg_added, 1)

            def add_parts(x_rows, h_rows, o):
                dve.tensor_tensor(o, x_rows, h_rows, ALU.add).then_inc(xh_made, 1)

            def update(k, p, ps, xh_rows, o):
                dve.wait_ge(projected, k + 1)
                ps = ps[0:p, 0:2 * C].rearrange("p (s c) -> p s c", s=2)
                dve.tensor_scalar(deg_max[0:p, :], ps[:, :, D], 1.0, None, ALU.max).then_inc(f_max, 1)
                dve.wait_ge(f_max, k + 1)
                dve.reciprocal(deg_inv[0:p, :], deg_max[0:p, :]).then_inc(f_inv, 1)
                dve.wait_ge(f_inv, k + 1)
                dve.scalar_tensor_tensor(out=upd[0:p, :, :], in0=ps[:, :, 0:D], scalar=0.0,
                                         in1=deg_inv[0:p, :].unsqueeze(2).broadcast_to([p, 2, D]),
                                         op0=ALU.max, op1=ALU.mult).then_inc(upd_made, 1)
                dve.wait_ge(xh_made, k + 1)
                dve.wait_ge(upd_made, k + 1)
                dve.tensor_tensor(o, upd[0:p, :, :], xh_rows, ALU.add).then_inc(res_ready, 1)

            def finish(k, p, loaded):
                dve.wait_ge(part_in, 32 * loaded + 32)
                add_parts(x_part[0:p, :, :], h_part[0:p, :, :], xh[0:p, :, :])
                update(k, p, ps_f, xh[0:p, :, :], res[0:p, :, :])

            def loop_step(i):
                for u in range(U):
                    n = i * U + u
                    one_hot(i, u)
                    message((u - 1) % U, n - 1)
                    add_window((u - 2) % U, n - 2)
                    if u == 4:
                        finish(i - LAG, FP, i - LAG)

            for i in range(LAG):
                for u in range(U):
                    n = i * U + u
                    one_hot(i, u)
                    if n >= 1:
                        message((u - 1) % U, n - 1)
                    if n == 2:
                        dve.wait_ge(acc_zero, 2)
                    if n >= 2:
                        add_window((u - 2) % U, n - 2)
                    if n == 1:
                        batch_statistics(2)
                    if n == 2:
                        batch_normalize(2)
                    if n == 3:
                        node_statistics(2)
                        normalize(2)
                        batch_statistics(3)
                    if n == 4:
                        batch_normalize(3)
                        node_statistics(3)
                    if n == 5:
                        normalize(3)
                        dve.wait_ge(weights_in, 16 * 4)
                        dve.tensor_copy(b_wide[:, :], b_col[:, 0:1].broadcast_to([F, P])).then_inc(b_wide_made, 1)
                    if n == 7:
                        dve.wait_ge(bias_multiplied, 1)
                        dve.tensor_tensor(b_last[:, 0:D], ps_bias[:, 0:D], b_up_all[:, :], ALU.add).then_inc(bias_made, 1)
                    if n >= 6 and n % 2 == 0 and n // 2 + 1 < len(BATCHES):
                        batch_statistics(n // 2 + 1)
                        batch_normalize(n // 2 + 1)
            dve.wait_ge(acc_zero, 2 + len(ZEROINGS))
            with dve.Fori(LAG, MIDDLE) as i:
                loop_step(i)
            dve.wait_ge(tail_in, 16 * 4)
            step(dve.tensor_copy(tail_dst_f[:, :], tail_dst[:, :]))
            step(dve.tensor_tensor(tail_rel[:, :], tail_dst_f[:, 0:1], tail_dst_f[:, 1:2], ALU.subtract))
            dve.tensor_scalar(tail_out[:, 0:1], tail_rel[:, :], float(WIN), None, ALU.is_ge)
            dve.tensor_scalar(tail_out[:, 1:2], tail_rel[:, :], 0.0, None, ALU.is_lt)
            step(dve.tensor_scalar(tail_onehot[:, :], iota[0:TAIL, 0:WIN], tail_rel[:, 0:1], None, ALU.is_equal))
            step(dve.tensor_tensor(misplaced[:, :], base_row[:, :], base_ok[:, :], ALU.not_equal))
            step(dve.tensor_reduce(n_misplaced[:, :], misplaced[:, :].rearrange("a (s c) -> a s c", s=2), AX.X, ALU.add))
            all_rel = rel_cols[:, :, :, :].rearrange("p i u j -> p (i u j)")
            step(dve.tensor_reduce(ext[:, 0:1], all_rel, AX.X, ALU.max))
            step(dve.tensor_reduce(ext[:, 1:2], all_rel, AX.X, ALU.min))
            dve.tensor_scalar(outside[:, 0:1], ext[:, 0:1], float(WIN), None, ALU.is_ge)
            dve.tensor_scalar(outside[:, 1:2], ext[:, 1:2], 0.0, None, ALU.is_lt).then_inc(out_cols, 1)
            dve.wait_ge(counted, 1)
            step(dve.tensor_reduce(n_outside_f[:, :], ps_cnt[0:1, 0:2], AX.X, ALU.add))
            dve.tensor_copy(n_outside[:, :], n_outside_f[:, :]).then_inc(flag_ready, 1)
            with dve.Fori(MIDDLE, STEPS) as i:
                loop_step(i)

            message(U - 1, CHUNKS - 1)
            add_window(U - 2, CHUNKS - 2)
            dve.wait_ge(more_in, 32 * EXTRA)
            for e in range(EXTRA):
                add_parts(more_x[e], more_h[e], more_xh[e])
            dve.wait_ge(multiplied, DONE)
            dve.tensor_tensor(msg[SLOT[0]][0:TAIL, 0, :], ps_m[SLOT[0]][0:TAIL, 0:F], b_neg[0:TAIL, :], ALU.max
                              ).then_inc(msg_ready, 1)
            add_window(U - 1, CHUNKS - 1)
            base = dve.value_load(base_ok[0:1, CHUNKS:CHUNKS + 1], min_val=0, max_val=N - 1)
            dve.wait_ge(summed, DONE)
            dve.wait_ge(added, CHUNKS)
            dve.wait_ge(deg_added, CHUNKS)
            z, deg = acc[:, 0, bass.ds(base, WIN)], acc[0:TAIL, 1, bass.ds(base, WIN)]
            dve.tensor_tensor(z, z, ps_w[:, 0:WIN], ALU.add).then_inc(added, 1)
            dve.tensor_tensor(deg, deg, tail_onehot[:, :], ALU.add).then_inc(deg_added, 1)

            dve.wait_ge(added, DONE)
            dve.wait_ge(deg_added, DONE)
            for e in range(EXTRA):
                if e:
                    dve.wait_ge(res_ready, LOOP_FIN + e)
                update(LOOP_FIN + e, NP, more_ps[e], more_xh[e], more_res[e])
            flag = dve.value_load(n_outside[0:1, 0:1], min_val=0, max_val=FLAG_MAX)
            with dve.If(flag > 0):
                dve.wait_ge(iota_wide, 1)
                dve.memset(acc[:, :, :], 0.0).then_inc(g_next, 1)
                dve.wait_ge(g_next, 1)
                with dve.Fori(0, GT) as t:
                    dve.wait_ge(g_in, 48 * t + 48)
                    dve.tensor_copy(g_dst_f[:, :], g_dst[:, :]).then_inc(g_dst_ready, 1)
                    dve.wait_ge(g_mult, t + 1)
                    dve.tensor_tensor(msg[0][0:GE, 0, :], ps_m[0][0:GE, 0:F], b_neg[0:GE, :], ALU.max).then_inc(g_msg, 1)
                    with dve.Fori(0, GB) as b:
                        m = t * GB + b
                        dve.wait_ge(g_dst_ready, m + t + 1)
                        dve.tensor_scalar(g_onehot, iota[0:GE, :], g_dst_f[:, 0:1], None, ALU.is_equal).then_inc(g_hot, 1)
                        dve.wait_ge(g_hot, m + 1)
                        dve.tensor_scalar(g_dst_f[:, :], g_dst_f[:, :], float(GN), None, ALU.subtract).then_inc(g_dst_ready, 1)
                        z, deg = acc[:, 0, bass.ds(b * GN, GN)], acc[0:GE, 1, bass.ds(b * GN, GN)]
                        dve.tensor_tensor(deg, deg, g_onehot, ALU.add).then_inc(g_added, 1)
                        dve.wait_ge(g_summed, m + 1)
                        dve.tensor_tensor(z, z, ps_g[:, 0:GN], ALU.add).then_inc(g_added, 1)
                        dve.wait_ge(g_added, 2 * m + 2)
                    dve.sem_inc(g_next, 1)
                dve.sem_inc(g_acc_done, 1)
                with dve.Fori(0, G_FIN) as b:
                    finish(b + (LOOP_FIN + EXTRA), NP, b + LOOP_FIN)
            with dve.Else():
                dve.nop()


_INS = ['x', 'src', 'dst', 'edge_attr_64', 'L0_gnn_W_pre', 'L0_gnn_b_pre', 'L0_gnn_W_up', 'L0_gnn_b_up']
_OUTS = [((12500, 64), 'float32')]


def kernel(**inputs):
    import numpy as _np
    import concourse.bacc as _bacc
    from concourse import mybir as _mybir
    from concourse.bass_utils import run_bass_kernel_spmd as _run

    nc = _bacc.Bacc("TRN2", target_bir_lowering=False, num_devices=1)
    arrays, args = {}, []
    for name in _INS:
        a = _np.ascontiguousarray(inputs[name])
        arrays[f"in_{name}_dram"] = a
        args.append(nc.dram_tensor(f"in_{name}_dram", a.shape, _mybir.dt.from_np(a.dtype), kind="ExternalInput").ap())
    for i, (shape, dtype) in enumerate(_OUTS):
        dt = _mybir.dt.from_np(_np.dtype(dtype))
        args.append(nc.dram_tensor(f"out_{i}_dram", shape, dt, kind="ExternalOutput").ap())
    gnn_kernel(nc, *args)
    r = _run(nc, [arrays], core_ids=[0])
    return r.results[0]["out_0_dram"]
```
